# Optimizing a Trainium2 kernel written in Bass

```python
import numpy as np
import jax
import jax.numpy as jnp

def _softmax(x, axis=-1):
    return jax.nn.softmax(x, axis=axis)

def _gelu(x):
    return jax.nn.gelu(x, approximate=True)

def _silu(x):
    return jax.nn.silu(x)

def _sigmoid(x):
    return jax.nn.sigmoid(x)

def _layernorm(x, axis=-1, eps=1e-05):
    m = jnp.mean(x, axis=axis, keepdims=True)
    v = jnp.var(x, axis=axis, keepdims=True)
    return (x - m) / jnp.sqrt(v + eps)

def _scatter_add(tgt, idx, src, axis=0):
    return tgt.at[idx].add(src)

def _segment_sum(src, seg, n):
    return jax.ops.segment_sum(src, seg, n)
kernel_name = 'mk_dlrm_tower_d1_rec_r8_d11b2b'

def setup_inputs(seed: int=0):
    np.random.seed(seed)
    _w = jnp.asarray

    def _rec_inputs():
        import jax
        import jax.numpy as jnp
        _tk = jax.random.key(seed)
        dense_ctx = jax.random.normal(jax.random.fold_in(_tk, 190), (512, 16), jnp.float32)
        ids = jnp.stack([jax.random.randint(jax.random.fold_in(_tk, 200 + f), (512,), 0, v, jnp.int32) for f, v in enumerate([1000, 1000, 1250, 125000, 1000, 125000, 1250, 125000, 1000, 125000, 125000, 125000, 125000, 12500, 125000, 1000, 12500, 1000, 1000, 1250, 1000, 1000, 1250, 1000, 1250, 1000, 1250, 12500, 1000, 12500, 12500, 12500])], axis=1)
        tbl_0 = 0.05 * jax.random.normal(jax.random.fold_in(_tk, 500 + 0), (1000, 16), jnp.float32)
        tbl_1 = 0.05 * jax.random.normal(jax.random.fold_in(_tk, 500 + 1), (1000, 16), jnp.float32)
        tbl_2 = 0.05 * jax.random.normal(jax.random.fold_in(_tk, 500 + 2), (1250, 16), jnp.float32)
        tbl_3 = 0.05 * jax.random.normal(jax.random.fold_in(_tk, 500 + 3), (125000, 16), jnp.float32)
        tbl_4 = 0.05 * jax.random.normal(jax.random.fold_in(_tk, 500 + 4), (1000, 16), jnp.float32)
        tbl_5 = 0.05 * jax.random.normal(jax.random.fold_in(_tk, 500 + 5), (125000, 16), jnp.float32)
        tbl_6 = 0.05 * jax.random.normal(jax.random.fold_in(_tk, 500 + 6), (1250, 16), jnp.float32)
        tbl_7 = 0.05 * jax.random.normal(jax.random.fold_in(_tk, 500 + 7), (125000, 16), jnp.float32)
        tbl_8 = 0.05 * jax.random.normal(jax.random.fold_in(_tk, 500 + 8), (1000, 16), jnp.float32)
        tbl_9 = 0.05 * jax.random.normal(jax.random.fold_in(_tk, 500 + 9), (125000, 16), jnp.float32)
        tbl_10 = 0.05 * jax.random.normal(jax.random.fold_in(_tk, 500 + 10), (125000, 16), jnp.float32)
        tbl_11 = 0.05 * jax.random.normal(jax.random.fold_in(_tk, 500 + 11), (125000, 16), jnp.float32)
        tbl_12 = 0.05 * jax.random.normal(jax.random.fold_in(_tk, 500 + 12), (125000, 16), jnp.float32)
        tbl_13 = 0.05 * jax.random.normal(jax.random.fold_in(_tk, 500 + 13), (12500, 16), jnp.float32)
        tbl_14 = 0.05 * jax.random.normal(jax.random.fold_in(_tk, 500 + 14), (125000, 16), jnp.float32)
        tbl_15 = 0.05 * jax.random.normal(jax.random.fold_in(_tk, 500 + 15), (1000, 16), jnp.float32)
        tbl_16 = 0.05 * jax.random.normal(jax.random.fold_in(_tk, 500 + 16), (12500, 16), jnp.float32)
        tbl_17 = 0.05 * jax.random.normal(jax.random.fold_in(_tk, 500 + 17), (1000, 16), jnp.float32)
        tbl_18 = 0.05 * jax.random.normal(jax.random.fold_in(_tk, 500 + 18), (1000, 16), jnp.float32)
        tbl_19 = 0.05 * jax.random.normal(jax.random.fold_in(_tk, 500 + 19), (1250, 16), jnp.float32)
        tbl_20 = 0.05 * jax.random.normal(jax.random.fold_in(_tk, 500 + 20), (1000, 16), jnp.float32)
        tbl_21 = 0.05 * jax.random.normal(jax.random.fold_in(_tk, 500 + 21), (1000, 16), jnp.float32)
        tbl_22 = 0.05 * jax.random.normal(jax.random.fold_in(_tk, 500 + 22), (1250, 16), jnp.float32)
        tbl_23 = 0.05 * jax.random.normal(jax.random.fold_in(_tk, 500 + 23), (1000, 16), jnp.float32)
        tbl_24 = 0.05 * jax.random.normal(jax.random.fold_in(_tk, 500 + 24), (1250, 16), jnp.float32)
        tbl_25 = 0.05 * jax.random.normal(jax.random.fold_in(_tk, 500 + 25), (1000, 16), jnp.float32)
        tbl_26 = 0.05 * jax.random.normal(jax.random.fold_in(_tk, 500 + 26), (1250, 16), jnp.float32)
        tbl_27 = 0.05 * jax.random.normal(jax.random.fold_in(_tk, 500 + 27), (12500, 16), jnp.float32)
        tbl_28 = 0.05 * jax.random.normal(jax.random.fold_in(_tk, 500 + 28), (1000, 16), jnp.float32)
        tbl_29 = 0.05 * jax.random.normal(jax.random.fold_in(_tk, 500 + 29), (12500, 16), jnp.float32)
        tbl_30 = 0.05 * jax.random.normal(jax.random.fold_in(_tk, 500 + 30), (12500, 16), jnp.float32)
        tbl_31 = 0.05 * jax.random.normal(jax.random.fold_in(_tk, 500 + 31), (12500, 16), jnp.float32)
        _rk = jax.random.fold_in(_tk, 7)
        W_top1 = 0.0693375 * jax.random.normal(jax.random.fold_in(_tk, 801), (208, 512), jnp.float32)
        W_top2 = 0.0441942 * jax.random.normal(jax.random.fold_in(_tk, 802), (512, 256), jnp.float32)
        W_top3 = 0.0625 * jax.random.normal(jax.random.fold_in(_tk, 803), (256, 1), jnp.float32)
        b_top1 = jnp.zeros((512,), jnp.float32)
        b_top2 = jnp.zeros((256,), jnp.float32)
        return (dense_ctx, ids, tbl_0, tbl_1, tbl_2, tbl_3, tbl_4, tbl_5, tbl_6, tbl_7, tbl_8, tbl_9, tbl_10, tbl_11, tbl_12, tbl_13, tbl_14, tbl_15, tbl_16, tbl_17, tbl_18, tbl_19, tbl_20, tbl_21, tbl_22, tbl_23, tbl_24, tbl_25, tbl_26, tbl_27, tbl_28, tbl_29, tbl_30, tbl_31, W_top1, b_top1, W_top2, b_top2, W_top3)
    dense_ctx, ids, tbl_0, tbl_1, tbl_2, tbl_3, tbl_4, tbl_5, tbl_6, tbl_7, tbl_8, tbl_9, tbl_10, tbl_11, tbl_12, tbl_13, tbl_14, tbl_15, tbl_16, tbl_17, tbl_18, tbl_19, tbl_20, tbl_21, tbl_22, tbl_23, tbl_24, tbl_25, tbl_26, tbl_27, tbl_28, tbl_29, tbl_30, tbl_31, W_top1, b_top1, W_top2, b_top2, W_top3 = _rec_inputs()

    def _L0_rec_setup():
        import jax, jax.numpy as jnp
        import numpy as np
        B, M, D = (2048, 32, 16)
        LAYERS = [64, 64, 64]
        key = jax.random.key(seed)
        ks = jax.random.split(key, 4)
        inp = {'embeddings': jax.random.normal(ks[0], (B, M, D), dtype=jnp.float32)}
        hk_1 = M
        for i, hk in enumerate(LAYERS):
            scale = (2.0 / (M * hk_1 + hk)) ** 0.5
            inp[f'W{i}'] = jax.random.normal(ks[i + 1], (M, hk_1, hk), dtype=jnp.float32) * scale
            hk_1 = hk
        return inp
    _L0_rec_all = _L0_rec_setup()
    _L0_rec_in = {k: v for k, v in _L0_rec_all.items() if k in ('W0', 'W1', 'W2')}
    del _L0_rec_all
    return {'dense_ctx': dense_ctx, 'ids': ids, 'tbl_0': tbl_0, 'tbl_1': tbl_1, 'tbl_2': tbl_2, 'tbl_3': tbl_3, 'tbl_4': tbl_4, 'tbl_5': tbl_5, 'tbl_6': tbl_6, 'tbl_7': tbl_7, 'tbl_8': tbl_8, 'tbl_9': tbl_9, 'tbl_10': tbl_10, 'tbl_11': tbl_11, 'tbl_12': tbl_12, 'tbl_13': tbl_13, 'tbl_14': tbl_14, 'tbl_15': tbl_15, 'tbl_16': tbl_16, 'tbl_17': tbl_17, 'tbl_18': tbl_18, 'tbl_19': tbl_19, 'tbl_20': tbl_20, 'tbl_21': tbl_21, 'tbl_22': tbl_22, 'tbl_23': tbl_23, 'tbl_24': tbl_24, 'tbl_25': tbl_25, 'tbl_26': tbl_26, 'tbl_27': tbl_27, 'tbl_28': tbl_28, 'tbl_29': tbl_29, 'tbl_30': tbl_30, 'tbl_31': tbl_31, 'W_top1': W_top1, 'b_top1': b_top1, 'W_top2': W_top2, 'b_top2': b_top2, 'W_top3': W_top3, 'L0_rec_W0': _L0_rec_in['W0'], 'L0_rec_W1': _L0_rec_in['W1'], 'L0_rec_W2': _L0_rec_in['W2']}

def reference(dense_ctx, ids, tbl_0, tbl_1, tbl_2, tbl_3, tbl_4, tbl_5, tbl_6, tbl_7, tbl_8, tbl_9, tbl_10, tbl_11, tbl_12, tbl_13, tbl_14, tbl_15, tbl_16, tbl_17, tbl_18, tbl_19, tbl_20, tbl_21, tbl_22, tbl_23, tbl_24, tbl_25, tbl_26, tbl_27, tbl_28, tbl_29, tbl_30, tbl_31, W_top1, b_top1, W_top2, b_top2, W_top3, L0_rec_W0, L0_rec_W1, L0_rec_W2):
    import jax
    import jax.numpy as jnp

    def _L0_rec_ref(embeddings, W0, W1, W2):
        import jax, jax.numpy as jnp
        import numpy as np
        B, M, D = (2048, 32, 16)
        LAYERS = [64, 64, 64]
        x0 = embeddings
        xk = x0
        outs = []
        for W in (W0, W1, W2):
            xk = jax.nn.relu(jnp.einsum('bmd,bhd,mhk->bkd', x0, xk, W))
            outs.append(jnp.sum(xk, axis=2))
        return jnp.concatenate(outs, axis=1)
    e = jnp.stack([tbl_0[ids[:, 0]], tbl_1[ids[:, 1]], tbl_2[ids[:, 2]], tbl_3[ids[:, 3]], tbl_4[ids[:, 4]], tbl_5[ids[:, 5]], tbl_6[ids[:, 6]], tbl_7[ids[:, 7]], tbl_8[ids[:, 8]], tbl_9[ids[:, 9]], tbl_10[ids[:, 10]], tbl_11[ids[:, 11]], tbl_12[ids[:, 12]], tbl_13[ids[:, 13]], tbl_14[ids[:, 14]], tbl_15[ids[:, 15]], tbl_16[ids[:, 16]], tbl_17[ids[:, 17]], tbl_18[ids[:, 18]], tbl_19[ids[:, 19]], tbl_20[ids[:, 20]], tbl_21[ids[:, 21]], tbl_22[ids[:, 22]], tbl_23[ids[:, 23]], tbl_24[ids[:, 24]], tbl_25[ids[:, 25]], tbl_26[ids[:, 26]], tbl_27[ids[:, 27]], tbl_28[ids[:, 28]], tbl_29[ids[:, 29]], tbl_30[ids[:, 30]], tbl_31[ids[:, 31]]], axis=1)
    z = _L0_rec_ref(e, L0_rec_W0, L0_rec_W1, L0_rec_W2)
    z = z.reshape(z.shape[0], -1)
    h = jnp.concatenate([z, dense_ctx], axis=1)
    h = jnp.maximum(h @ W_top1 + b_top1, 0.0)
    h = jnp.maximum(h @ W_top2 + b_top2, 0.0)
    y = h @ W_top3
    return y

_drawn_inputs = setup_inputs


def setup_inputs(seed=0):
    import zlib

    import numpy as np

    out = dict(_drawn_inputs(seed))
    spreads = {'b_top1': (0.0, 2.0), 'b_top2': (0.0, 0.8)}
    factors = {'tbl_0': 8.0,
     'tbl_1': 8.0,
     'tbl_2': 8.0,
     'tbl_3': 8.0,
     'tbl_4': 8.0,
     'tbl_5': 8.0,
     'tbl_6': 8.0,
     'tbl_7': 8.0,
     'tbl_8': 8.0,
     'tbl_9': 8.0,
     'tbl_10': 8.0,
     'tbl_11': 8.0,
     'tbl_12': 8.0,
     'tbl_13': 8.0,
     'tbl_14': 8.0,
     'tbl_15': 8.0,
     'tbl_16': 8.0,
     'tbl_17': 8.0,
     'tbl_18': 8.0,
     'tbl_19': 8.0,
     'tbl_20': 8.0,
     'tbl_21': 8.0,
     'tbl_22': 8.0,
     'tbl_23': 8.0,
     'tbl_24': 8.0,
     'tbl_25': 8.0,
     'tbl_26': 8.0,
     'tbl_27': 8.0,
     'tbl_28': 8.0,
     'tbl_29': 8.0,
     'tbl_30': 8.0,
     'tbl_31': 8.0,
     'L0_rec_W0': 3.598,
     'L0_rec_W1': 8.0,
     'L0_rec_W2': 8.0,
     'dense_ctx': 7.146}
    for name, (base, spread) in spreads.items():
        noise = np.random.default_rng([zlib.crc32(name.encode()), seed]).standard_normal(out[name].shape)
        drawn = base * np.exp(spread * noise) if base else spread * noise
        out[name] = jnp.asarray(drawn.astype(out[name].dtype))
    for name, factor in factors.items():
        out[name] = (out[name] * factor).astype(out[name].dtype)
    return out
```

```python
from contextlib import ExitStack

import concourse.bass as bass
from concourse import mybir

F32 = mybir.dt.float32
I32 = mybir.dt.int32
ALU = mybir.AluOpType
ACT = mybir.ActivationFunctionType
AX = mybir.AxisListType

BATCH, FIELDS, DIM = 512, 32, 16
HID = 64
P = 128
TILES = BATCH // P
TCOLS = DIM * P
CH = 512
PC = 2 * CH
KT = FIELDS * HID // P
GR = 4
UNIT = 2
UPJ = KT // UNIT
L0U = 2
DENSE = 16
TOP1, TOP2 = 512, 256
M1, M2 = TOP1 // P, TOP2 // P
X0ROWS = FIELDS + DIM

ZR = 3
PZR = 2

JOBS = ("L1a", "L0b", "L2a", "L1b", "L0c", "L2b")
POOL_UNITS = {"L1a": 1, "L2a": 1, "L1b": 2, "L2b": 2}
POOL_UNITS_LAST = {"L1a": 2, "L2a": 2, "L1b": 2, "L2b": 2}
POOL_AT = {0: (), 1: (5,), 2: (4, 7), 3: (3, 5, 7)}
GATHERS = {"L1a": 20, "L2a": 12, "L1b": 0, "L2b": 0}
GRANULES = {1: (0, 1, 2, 3), 2: (2, 3, 0, 1)}


def layer(job):
    return int(job[1])


class Counts:

    def __init__(self, last):
        self.last = last
        self.jobs = [j for j in JOBS if not (last and j == "L0c")]
        self.share = POOL_UNITS_LAST if last else POOL_UNITS
        self.dve, self.pool, self.mm, at, pat, mat = {}, {}, {}, 0, 0, 0
        self.dve_ends, self.pool_ends = [], []
        for j in self.jobs:
            self.dve[j], self.pool[j] = at, pat
            self.mm[j] = mat
            if layer(j) == 0:
                self.dve_ends += [mat + n + 1 for n in range(L0U)]
                mat += L0U + 1
            else:
                for pos in range(UPJ):
                    (self.pool_ends if pos in POOL_AT[self.share[j]] else self.dve_ends).append(mat + pos + 1)
                mat += UPJ
            at += L0U if layer(j) == 0 else UPJ - self.share[j]
            pat += self.share.get(j, 0)
        self.dve_units, self.pool_units, self.mm_units = at, pat, mat

    def pool_at(self, job):
        return POOL_AT[self.share[job]]

    def units(self, job):
        n = {True: 0, False: 0}
        for pos in range(UPJ):
            on_pool = pos in self.pool_at(job)
            yield pos, GRANULES[layer(job)][pos // 2], pos % 2, on_pool, n[on_pool]
            n[on_pool] += 1

    def job_number(self, job, i):
        return 6 * i + 2 + self.jobs.index(job)

    def dve_before(self, job, i):
        return L0U + i * BODY.dve_units + self.dve[job]

    def pool_before(self, job, i):
        return i * BODY.pool_units + self.pool[job]

    def used(self, job, i, granule):
        return self.mm_before(job, i) + 2 * GRANULES[layer(job)].index(granule) + 2

    def job_end(self, job, i):
        n = L0U if layer(job) == 0 else UPJ - self.share[job]
        return self.dve_before(job, i) + n, self.pool_before(job, i) + self.share.get(job, 0)

    def mm_before(self, job, i):
        return L0U + 1 + i * BODY.mm_units + self.mm[job]

    def mm_end(self, job, i):
        return self.mm_before(job, i) + (L0U + 1 if layer(job) == 0 else UPJ)

    def mm_when_free(self, job, n, on_pool, i):
        mine, before, ring = (self.pool_ends, BODY.pool_ends, PZR) if on_pool else (self.dve_ends, BODY.dve_ends, ZR)
        u = (self.pool if on_pool else self.dve)[job] + n - ring
        off = mine[u] if u >= 0 else max(before[u] - BODY.mm_units, -L0U)
        return L0U + 1 + i * BODY.mm_units + off


BODY, LAST = Counts(False), Counts(True)
assert BODY.dve_units % ZR == 0 and BODY.pool_units % PZR == 0
assert sum(GATHERS.values()) == FIELDS


def pair_of(job, i):
    return 2 * i + "abc".index(job[2])


def program(nc, dense_ctx, ids, tables, w_top1, b_top1, w_top2, b_top2, w_top3, w0, w1, w2, out):
    ctx = ExitStack()
    with ctx:
        def sb(name, shape, dt=F32):
            return ctx.enter_context(nc.sbuf_tensor(name, shape, dt))

        def sem(name):
            return ctx.enter_context(nc.semaphore(name))

        x0_dram = nc.dram_tensor("x0_dram", (TILES, X0ROWS, TCOLS), F32)
        w0_h2 = nc.dram_tensor("w0_h2", (FIELDS, 2 * FIELDS, HID), F32)
        w0_m2 = nc.dram_tensor("w0_m2", (X0ROWS, FIELDS, HID), F32)

        idx = sb("idx", [P, FIELDS], I32)
        emb = sb("emb", [P, FIELDS * DIM])
        dctx = sb("dctx", [P, DENSE])
        ident = sb("ident", [P, P])
        x0t = sb("x0t", [P, 4, P])
        rep = sb("rep", [P, PC])
        shf = sb("shf", [P, 4, PC])
        bc = sb("bc", [P, 6, GR, PC])
        z = sb("z", [P, ZR, UNIT, PC])
        pz = sb("pz", [P, PZR, UNIT, PC])
        z16 = sb("z16", [P, PC])
        xdup = sb("xdup", [P, 2, PC])
        xs = sb("xs", [P, 2, CH])
        zp = sb("zp", [P, 3, 2, P])
        zin = sb("zin", [P, 3, P])
        dense_t = sb("dense_t", [DENSE, P])
        h1 = sb("h1", [P, M1, P])
        h2 = sb("h2", [P, M2, P])
        yrow = sb("yrow", [1, P])
        w0s = sb("w0s", [P, 4, HID])
        w16s = sb("w16s", [P, HID])
        w0a = pz[:, 1, 0, 0:4 * HID].rearrange("p (t k) -> p t k", k=HID)
        w0b = pz[:, 1, 0, 4 * HID:8 * HID].rearrange("p (t k) -> p t k", k=HID)
        w16a = pz[0:DIM, 1, 0, 8 * HID:9 * HID]
        w16b = pz[0:DIM, 1, 0, 9 * HID:10 * HID]
        wl = sb("wl", [P, 2, KT, HID])
        wt1 = sb("wt1", [P, 3, TOP1])
        wt1d = sb("wt1d", [DENSE, TOP1])
        wt2 = sb("wt2", [P, M1, TOP2])
        wt3 = sb("wt3", [P, M2])
        bt1 = sb("bt1", [P, M1])
        bt2 = sb("bt2", [P, M2])

        y_ps = ctx.enter_context(nc.psum_tensor("y_ps", [P, 2, CH], F32))
        x_ps = ctx.enter_context(nc.psum_tensor("x_ps", [P, 2, PC], F32))
        t_ps = ctx.enter_context(nc.psum_tensor("t_ps", [P, 4, P], F32))
        m_ps = ctx.enter_context(nc.psum_tensor("m_ps", [P, 4, P], F32))

        ids_loaded = sem("ids_loaded")
        dctx_loaded = sem("dctx_loaded")
        gathered = sem("gathered")
        x0_transposed = sem("x0_transposed")
        x0t_ready = sem("x0t_ready")
        x0_stored = sem("x0_stored")
        l0_loaded = sem("l0_loaded")
        bc_loaded = [sem(f"bc_loaded{n}") for n in range(6)]
        z_made = sem("z_made")
        z16_made = sem("z16_made")
        pz_made = sem("pz_made")
        x_ready = sem("x_ready")
        xdup_ready = sem("xdup_ready")
        xs_ready = sem("xs_ready")
        dsum_done = sem("dsum_done")
        zin_ready = sem("zin_ready")
        h1_mm = sem("h1_mm")
        h1_ready = sem("h1_ready")
        h2_mm = sem("h2_mm")
        h2_ready = sem("h2_ready")
        y_mm = sem("y_mm")
        contracted = sem("contracted")
        y_copied = sem("y_copied")
        y_stored = sem("y_stored")
        dense_transposed = sem("dense_transposed")
        dense_ready = sem("dense_ready")
        zeroed = sem("zeroed")
        ident_ready = sem("ident_ready")
        w0_copied = sem("w0_copied")
        w0_loaded = sem("w0_loaded")
        w0_summed = sem("w0_summed")
        w_loaded = sem("w_loaded")
        wt_loaded = sem("wt_loaded")

        def bc_slot(pair_parity, granule):
            return granule + (4 * pair_parity if granule < 2 else 0)

        def bc_count(job, i, granule):
            second = "abc".index(job[2])
            return 32 * (i + 1) if granule < 2 else 32 * (2 * i + second + 1)

        def parity(job):
            return "abc".index(job[2]) % 2

        zero_list = [zp[:], zin[:], z16[:], w16s[:]]

        block = ctx.enter_context(nc.Block())

        @block.sync
        def _(sp):
            def load_l0(base):
                for j in range(4):
                    rows = slice(FIELDS * j, FIELDS * (j + 1))
                    sp.dma_start(rep[rows, :], bass.AP(x0_dram, base, [[TCOLS, FIELDS], [1, PC]])).then_inc(l0_loaded, 16)
                    sp.dma_start(shf[rows, :, :], bass.AP(x0_dram, base + j * TCOLS if j else base, [[TCOLS, FIELDS], [4 * TCOLS, 4], [1, PC]])).then_inc(l0_loaded, 16)
                sp.dma_start(z16[0:DIM, :], bass.AP(x0_dram, base + DIM * TCOLS, [[TCOLS, DIM], [1, PC]])).then_inc(l0_loaded, 16)

            def load_bc(base, half, granule):
                slot = bc_slot(half, granule)
                for j in range(2):
                    sp.dma_start(bc[HID * j:HID * (j + 1), slot, :, :],
                                 bass.AP(x0_dram, base + j * TCOLS if j else base, [[0, HID], [2 * TCOLS, GR], [1, PC]])).then_inc(bc_loaded[slot], 16)

            def start(tile, half, granule=0):
                return tile * (X0ROWS * TCOLS) + (half * PC + 2 * GR * granule * TCOLS)

            sp.dma_start(idx[:, :], ids[0:P, :]).then_inc(ids_loaded, 16)
            sp.dma_start(w0_h2[:, 0:FIELDS, :], w0).then_inc(w0_copied, 16)
            sp.dma_start(w0_h2[:, FIELDS:2 * FIELDS, :], w0).then_inc(w0_copied, 16)
            sp.dma_start(w0_m2[0:FIELDS, :, :], w0).then_inc(w0_copied, 16)
            sp.dma_start(w0_m2[FIELDS:X0ROWS, :, :], w0[0:DIM, :, :]).then_inc(w0_copied, 16)
            for n, w in enumerate((w1, w2)):
                for j in range(2):
                    sp.dma_start(wl[HID * j:HID * (j + 1), n, :, :],
                                 w.rearrange("(t j) h k -> j h t k", j=2)[j]).then_inc(w_loaded, 16)
            sp.wait_ge(w0_copied, 4 * 16)
            for j in range(4):
                rows = slice(FIELDS * j, FIELDS * (j + 1))
                sp.dma_start(w0a[rows, :, :], bass.AP(w0_h2, j * HID, [[(2 * FIELDS + 1) * HID, FIELDS], [4 * HID, 4], [1, HID]])).then_inc(w0_loaded, 16)
                sp.dma_start(w0b[rows, :, :], bass.AP(w0_m2, j * FIELDS * HID, [[(FIELDS + 1) * HID, FIELDS], [4 * FIELDS * HID, 4], [1, HID]])).then_inc(w0_loaded, 16)
            sp.dma_start(w16a, bass.AP(w0_h2, DIM * HID, [[(2 * FIELDS + 1) * HID, DIM], [1, HID]])).then_inc(w0_loaded, 16)
            sp.dma_start(w16b, bass.AP(w0_m2, DIM * FIELDS * HID, [[(FIELDS + 1) * HID, DIM], [1, HID]])).then_inc(w0_loaded, 16)
            for c in range(2):
                sp.dma_start(wt1[HID * c:HID * (c + 1), :, :], w_top1[0:3 * HID, :].rearrange("(l k) n -> k l n", l=3)).then_inc(wt_loaded, 16)
            sp.dma_start(wt1d[:, :], w_top1[3 * HID:3 * HID + DENSE, :]).then_inc(wt_loaded, 16)
            sp.dma_start(wt2[:, :, :], w_top2.rearrange("(t p) n -> p t n", p=P)).then_inc(wt_loaded, 16)
            with nc.allow_non_contiguous_dma(reason="a few hundred words, once"):
                sp.dma_start(wt3[:, :], w_top3.rearrange("(t p) o -> p (t o)", p=P)).then_inc(wt_loaded, 16)
                sp.dma_start(bt1[:, :], b_top1.rearrange("(t p) -> p t", p=P)).then_inc(wt_loaded, 16)
                sp.dma_start(bt2[:, :], b_top2.rearrange("(t p) -> p t", p=P)).then_inc(wt_loaded, 16)
            sp.wait_ge(x0_stored, 2 * 16)
            sp.wait_ge(zeroed, 1 + len(zero_list))
            load_l0(start(0, 0))
            for g in range(4):
                load_bc(start(0, 0, g), 0, g)

            def body(i, c):
                if not c.last:
                    sp.wait_ge(gathered, 16 * FIELDS * (i + 1))
                    sp.dma_start(idx[:, :], ids[bass.ds((i + 1) * P, P), :]).then_inc(ids_loaded, 16)
                sp.wait_ge(contracted, c.mm_before("L1a", i))
                sp.dma_start(dctx[:, :], dense_ctx[bass.ds(i * P, P), :]).then_inc(dctx_loaded, 16)
                load_l0(start(i, 1))
                load_bc(start(i, 1, 0), 1, 0)
                load_bc(start(i, 1, 1), 1, 1)
                for g in (2, 3):
                    sp.wait_ge(contracted, c.used("L2a", i, g))
                    load_bc(start(i, 1, g), 1, g)
                if c.last:
                    return
                sp.wait_ge(x0_stored, 2 * 16 * (i + 2))
                load_l0(start(i + 1, 0))
                load_bc(start(i + 1, 0, 0), 0, 0)
                load_bc(start(i + 1, 0, 1), 0, 1)
                for g in (2, 3):
                    sp.wait_ge(contracted, c.used("L2b", i, g))
                    load_bc(start(i + 1, 0, g), 0, g)

            with sp.Fori(0, TILES - 1) as i:
                body(i, BODY)
            body(TILES - 1, LAST)
            sp.wait_ge(y_stored, 16 * (TILES + 1))

        @block.gpsimd
        def _(pool):
            pool.memset(ident[:, :], 0.0).then_inc(zeroed, 1)
            for t in zero_list:
                pool.memset(t, 0.0).then_inc(zeroed, 1)
            pool.memset(xs[:, 1, :], 0.0).then_inc(xs_ready, 1)
            pool.memset(dense_t[:, :], 0.0).then_inc(dense_ready, 1)
            pool.wait_ge(zeroed, 1)
            pool.affine_select(out=ident[:, :], in_=ident[:, :], compare_op=ALU.not_equal, fill=1.0,
                               base=0, pattern=[[-1, P]], channel_multiplier=1).then_inc(ident_ready, 1)

            def gather(t0, t1):
                for t in range(t0, t1):
                    pool.indirect_dma_start(out=emb[:, DIM * t:DIM * (t + 1)], out_offset=None, in_=tables[t],
                                            in_offset=bass.IndirectOffsetOnAxis(ap=idx[:, t:t + 1], axis=0)).then_inc(gathered, 16)

            pool.wait_ge(ids_loaded, 16)
            gather(0, FIELDS)

            def body(i, c):
                got = 0
                if not c.last:
                    pool.wait_ge(ids_loaded, 16 * (i + 2))
                    pool.wait_ge(x0_transposed, i + 1)
                for job in ("L1a", "L2a", "L1b", "L2b"):
                    src = layer(job) - 1
                    if c.share[job]:
                        pool.wait_ge(xdup_ready, 2 * pair_of(job, i) + src + 1)
                    for _, g, half, on_pool, n in c.units(job):
                        if not on_pool:
                            continue
                        slot = (c.pool[job] + n) % PZR
                        bslot = bc_slot(parity(job), g)
                        pool.wait_ge(bc_loaded[bslot], bc_count(job, i, g))
                        pool.wait_ge(contracted, c.mm_when_free(job, n, True, i))
                        pool.tensor_tensor(out=pz[:, slot, :, :],
                                           in0=xdup[:, src, None, :].broadcast_to([P, UNIT, PC]),
                                           in1=bc[:, bslot, UNIT * half:UNIT * (half + 1), :], op=ALU.mult).then_inc(pz_made, 1)
                    if not c.last and GATHERS[job]:
                        gather(got, got + GATHERS[job])
                        got += GATHERS[job]

            with pool.Fori(0, TILES - 1) as i:
                body(i, BODY)
            body(TILES - 1, LAST)

        @block.vector
        def _(dve):
            def l0_units(p, slot0, free):
                dve.wait_ge(l0_loaded, 9 * 16 * (p + 1))
                for n in range(L0U):
                    if free:
                        dve.wait_ge(contracted, free[n])
                    dve.tensor_tensor(out=z[:, (slot0 + n) % ZR, :, :], in0=rep[:, None, :].broadcast_to([P, UNIT, PC]),
                                      in1=shf[:, UNIT * n:UNIT * (n + 1), :], op=ALU.mult).then_inc(z_made, 1)
                dve.tensor_tensor(out=z16[0:DIM, :], in0=rep[0:DIM, :], in1=z16[0:DIM, :], op=ALU.mult).then_inc(z16_made, 1)

            def dsum(number, par, lay, pr):
                dve.wait_ge(xs_ready, number + 1)
                dve.tensor_reduce(out=zp[:, lay, pr, :], in_=xs[:, par, :].rearrange("p (d b) -> p b d", b=P),
                                  op=ALU.add, axis=AX.X).then_inc(dsum_done, 1)

            def zadd(lay, number, mlps):
                dve.wait_ge(dsum_done, number + 1)
                if mlps is not None:
                    dve.wait_ge(h1_mm, mlps)
                dve.tensor_tensor(out=zin[:, lay, :], in0=zp[:, lay, 0, :], in1=zp[:, lay, 1, :], op=ALU.add).then_inc(zin_ready, 1)

            dve.wait_ge(zeroed, 1 + len(zero_list))
            dve.wait_ge(w0_loaded, 10 * 16)
            dve.tensor_copy(w0s[0:FIELDS, 0, :], w0a[0:FIELDS, 0, :]).then_inc(w0_summed, 1)
            dve.tensor_tensor(out=w0s[0:FIELDS, 1:4, :], in0=w0a[0:FIELDS, 1:4, :], in1=w0b[0:FIELDS, 1:4, :], op=ALU.add).then_inc(w0_summed, 1)
            for j in range(1, 4):
                rows = slice(FIELDS * j, FIELDS * (j + 1))
                dve.tensor_tensor(out=w0s[rows, :, :], in0=w0a[rows, :, :], in1=w0b[rows, :, :], op=ALU.add).then_inc(w0_summed, 1)
            dve.tensor_tensor(out=w16s[0:DIM, :], in0=w16a, in1=w16b, op=ALU.add).then_inc(w0_summed, 1)
            l0_units(0, 0, None)
            dsum(1, 0, 0, 0)

            def body(i, c):
                def units(job, hooks):
                    if layer(job) == 0:
                        l0_units(pair_of(job, i), L0U + c.dve[job], [c.mm_when_free(job, n, False, i) for n in range(L0U)])
                        return
                    src = layer(job) - 1
                    dve.wait_ge(x_ready, 2 * pair_of(job, i) + src + 1)
                    for _, g, half, on_pool, n in c.units(job):
                        if on_pool:
                            continue
                        if n in hooks:
                            hooks[n]()
                        bslot = bc_slot(parity(job), g)
                        dve.wait_ge(bc_loaded[bslot], bc_count(job, i, g))
                        dve.wait_ge(contracted, c.mm_when_free(job, n, False, i))
                        dve.tensor_tensor(out=z[:, (L0U + c.dve[job] + n) % ZR, :, :],
                                          in0=x_ps[:, src, None, :].broadcast_to([P, UNIT, PC]),
                                          in1=bc[:, bslot, UNIT * half:UNIT * (half + 1), :], op=ALU.mult).then_inc(z_made, 1)

                def sums(job, lay, pr, mlps=None):
                    def run():
                        number = c.job_number(job, i)
                        dsum(number, c.jobs.index(job) % 2, lay, pr)
                        if mlps is not None:
                            zadd(lay, number, mlps)
                    return run

                def sums_before():
                    dsum(6 * i + 1, 1, 2, 1)
                    zadd(2, 6 * i + 1, None)

                units("L1a", {3: sums_before})
                units("L0b", {})
                units("L2a", {2: sums("L1a", 1, 0), 5: sums("L0b", 0, 1, i + 1)})
                units("L1b", {3: sums("L2a", 2, 0)})
                if not c.last:
                    units("L0c", {})
                    units("L2b", {2: sums("L1b", 1, 1, i + 1), 5: sums("L0c", 0, 0)})
                else:
                    units("L2b", {3: sums("L1b", 1, 1, i + 1)})
                    sums("L2b", 2, 1, i + 1)()

            with dve.Fori(0, TILES - 1) as i:
                body(i, BODY)
            body(TILES - 1, LAST)

        @block.scalar
        def _(act):
            def spread(bank, src, psum_first=True):
                both = [(x_ps, x_ready), (xdup, xdup_ready)]
                for dst, done in both if psum_first else both[::-1]:
                    for c in range(2):
                        for half in range(2):
                            op = act.activation(dst[HID * half:HID * (half + 1), src, CH * c:CH * (c + 1)],
                                                y_ps[HID * c:HID * (c + 1), bank, :], ACT.Relu)
                    op.then_inc(done, 1)

            def keep(bank, par):
                act.activation(xs[:, par, :], y_ps[:, bank, :], ACT.Relu).then_inc(xs_ready, 1)

            def copy_x0(tile):
                act.wait_ge(x0_transposed, tile + 1)
                act.activation(x0t[:, :, :], t_ps[:, :, :], ACT.Copy).then_inc(x0t_ready, 1)

            def store_x0(tile):
                act.wait_ge(x0t_ready, tile + 1)
                for row, quarters in ((0, 4), (FIELDS, 2)):
                    dst = bass.AP(x0_dram, tile * (X0ROWS * TCOLS) + row * TCOLS, [[P, P], [8 * TCOLS, quarters], [1, P]])
                    act.dma_start(dst, x0t[:, 0:quarters, :]).then_inc(x0_stored, 16)

            def evac(i, c, job):
                number = c.job_number(job, i)
                par = c.jobs.index(job) % 2
                act.wait_ge(contracted, c.mm_end(job, i))
                if layer(job) < 2:
                    spread(par, layer(job))
                act.wait_ge(dsum_done, number - 1)
                keep(par, par)

            def top1(n):
                act.wait_ge(h1_mm, n + 1)
                for m in range(M1):
                    op = act.activation(h1[:, m, :], m_ps[:, m, :], ACT.Relu, bias=bt1[:, m:m + 1])
                op.then_inc(h1_ready, 1)

            def top2(n):
                act.wait_ge(h2_mm, n + 1)
                for m in range(M2):
                    op = act.activation(h2[:, m, :], m_ps[:, m, :], ACT.Relu, bias=bt2[:, m:m + 1])
                op.then_inc(h2_ready, 1)

            def top3(n, block_row):
                act.wait_ge(y_mm, n + 1)
                act.activation(yrow[:, :], m_ps[0:1, 0, :], ACT.Copy).then_inc(y_copied, 1)
                act.wait_ge(y_copied, n + 1)
                act.dma_start(out[bass.ds(block_row * P, P), :].rearrange("b o -> o b"), yrow[:, :]).then_inc(y_stored, 16)

            copy_x0(0)
            store_x0(0)
            act.wait_ge(zeroed, 1 + len(zero_list))
            act.wait_ge(wt_loaded, 7 * 16)
            act.wait_ge(contracted, L0U + 1)
            keep(0, 0)
            spread(0, 0, psum_first=False)

            def body(i, c):
                evac(i, c, "L1a")
                top1(i)
                evac(i, c, "L0b")
                top2(i)
                evac(i, c, "L2a")
                top3(i, (i + TILES - 1) % TILES)
                act.wait_ge(dense_transposed, i + 1)
                act.wait_ge(h1_mm, i + 1)
                act.activation(dense_t[:, :], m_ps[0:DENSE, 1, :], ACT.Copy).then_inc(dense_ready, 1)
                if not c.last:
                    act.wait_ge(x0_stored, 2 * 16 * (i + 1))
                    copy_x0(i + 1)
                    store_x0(i + 1)
                evac(i, c, "L1b")
                if not c.last:
                    evac(i, c, "L0c")
                evac(i, c, "L2b")
                act.wait_ge(y_stored, 16 * (i + 1))

            with act.Fori(0, TILES - 1) as i:
                body(i, BODY)
            body(TILES - 1, LAST)
            top1(TILES)
            top2(TILES)
            top3(TILES, TILES - 1)

        @block.tensor
        def _(pe):
            def tile_mms(bank, weights, products, start, stop):
                for c in range(2):
                    op = pe.matmul(y_ps[HID * c:HID * (c + 1), bank, :], weights, products[:, CH * c:CH * (c + 1)],
                                   start=start, stop=stop)
                return op

            def l0_job(first, p, slot0, bank):
                for n in range(L0U):
                    pe.wait_ge(z_made, first + n + 1)
                    for t in range(UNIT):
                        op = tile_mms(bank, w0s[:, UNIT * n + t, :], z[:, (slot0 + n) % ZR, t, :], n == 0 and t == 0, False)
                    op.then_inc(contracted, 1)
                pe.wait_ge(z16_made, p + 1)
                tile_mms(bank, w16s[:, :], z16[:, :], False, True).then_inc(contracted, 1)

            def transposes(tile):
                pe.wait_ge(gathered, 16 * FIELDS * (tile + 1))
                pe.wait_ge(x0t_ready, tile)
                for q in range(4):
                    op = pe.transpose(t_ps[:, q, :], emb[:, P * q:P * (q + 1)], ident[:, :])
                op.then_inc(x0_transposed, 1)

            pe.wait_ge(ident_ready, 1)
            pe.wait_ge(zeroed, 1 + len(zero_list))
            transposes(0)
            pe.wait_ge(w0_summed, 6)
            pe.wait_ge(w_loaded, 4 * 16)
            l0_job(0, 0, 0, 0)
            pe.wait_ge(wt_loaded, 7 * 16)

            def mlp1(n):
                pe.wait_ge(zin_ready, 3 * n + 1)
                pe.wait_ge(dense_ready, n + 1)
                for m in range(M1):
                    cols = slice(P * m, P * (m + 1))
                    for lay in range(3):
                        pe.matmul(m_ps[:, m, :], wt1[:, lay, cols], zin[:, lay, :], start=lay == 0, stop=False)
                    op = pe.matmul(m_ps[:, m, :], wt1d[:, cols], dense_t[:, :], start=False, stop=True)
                op.then_inc(h1_mm, 1)

            def mlp2(n):
                pe.wait_ge(h1_ready, n + 1)
                for m in range(M2):
                    for t in range(M1):
                        op = pe.matmul(m_ps[:, m, :], wt2[:, t, P * m:P * (m + 1)], h1[:, t, :], start=t == 0, stop=t == M1 - 1)
                op.then_inc(h2_mm, 1)

            def mlp3(n):
                pe.wait_ge(h2_ready, n + 1)
                for t in range(M2):
                    op = pe.matmul(m_ps[0:1, 0, :], wt3[:, t:t + 1], h2[:, t, :], start=t == 0, stop=t == M2 - 1)
                op.then_inc(y_mm, 1)

            def dense(i):
                pe.wait_ge(dctx_loaded, 16 * (i + 1))
                pe.wait_ge(y_copied, i + 1)
                pe.transpose(m_ps[0:DENSE, 1, :], dctx[:, :], ident[:, :]).then_inc(dense_transposed, 1)

            def body(i, c):
                def job(name, middle=None):
                    number = c.job_number(name, i)
                    bank = c.jobs.index(name) % 2
                    pe.wait_ge(xs_ready, number - 1)
                    if layer(name) == 0:
                        l0_job(c.dve_before(name, i), pair_of(name, i), L0U + c.dve[name], bank)
                        return
                    for pos, g, half, on_pool, n in c.units(name):
                        if pos == 4 and middle:
                            middle()
                        if on_pool:
                            pe.wait_ge(pz_made, c.pool_before(name, i) + n + 1)
                            src = pz[:, (c.pool[name] + n) % PZR, :, :]
                        else:
                            pe.wait_ge(z_made, c.dve_before(name, i) + n + 1)
                            src = z[:, (L0U + c.dve[name] + n) % ZR, :, :]
                        for t in range(UNIT):
                            op = tile_mms(bank, wl[:, layer(name) - 1, GR * g + UNIT * half + t, :], src[:, t, :],
                                          pos == 0 and t == 0, pos == UPJ - 1 and t == UNIT - 1)
                        op.then_inc(contracted, 1)

                def prepare():
                    dense(i)
                    if not c.last:
                        transposes(i + 1)

                job("L1a")
                mlp1(i)
                job("L0b")
                mlp2(i)
                job("L2a")
                mlp3(i)
                job("L1b", middle=prepare)
                if not c.last:
                    job("L0c")
                job("L2b")

            with pe.Fori(0, TILES - 1) as i:
                body(i, BODY)
            body(TILES - 1, LAST)
            mlp1(TILES)
            mlp2(TILES)
            mlp3(TILES)


def kernel(**inputs):
    import numpy as np
    import concourse.bacc as bacc
    from concourse.bass_utils import run_bass_kernel_spmd

    nc = bacc.Bacc("TRN2", target_bir_lowering=False, num_devices=1)
    arrays, args = {}, {}
    for name, value in inputs.items():
        a = np.ascontiguousarray(value)
        arrays[f"in_{name}"] = a
        args[name] = nc.dram_tensor(f"in_{name}", a.shape, mybir.dt.from_np(a.dtype), kind="ExternalInput").ap()
    out = nc.dram_tensor("out_0", (BATCH, 1), F32, kind="ExternalOutput").ap()
    program(nc, args["dense_ctx"], args["ids"], [args[f"tbl_{t}"] for t in range(FIELDS)],
            args["W_top1"], args["b_top1"], args["W_top2"], args["b_top2"], args["W_top3"],
            args["L0_rec_W0"], args["L0_rec_W1"], args["L0_rec_W2"], out)
    return run_bass_kernel_spmd(nc, [arrays], core_ids=[0]).results[0]["out_0"]
```

```python
from contextlib import ExitStack

import concourse.bass as bass
from concourse import mybir

F32 = mybir.dt.float32
I32 = mybir.dt.int32
ALU = mybir.AluOpType
ACT = mybir.ActivationFunctionType
AX = mybir.AxisListType

BATCH, FIELDS, DIM = 512, 32, 16
HID = 64
P = 128
TILES = BATCH // P
TCOLS = DIM * P
CH = 512
PC = 2 * CH
KT = FIELDS * HID // P
GR = 4
UNIT = 2
UPJ = KT // UNIT
L0U = 2
DENSE = 16
HOT = ((18, 20, 22, 24), (19, 21, 23, 25), (0, 2), (17, 26), (1,))
HP, HOT_C = 125, 10
HOT_TABLES = [t for group in HOT for t in group]
COLD = [t for t in range(FIELDS) if t not in HOT_TABLES]


def hot_place(t):
    return 2 * DIM * (t % 8 // 2), t // 8, t % 2


assert all(len({hot_place(t)[0] for t in group}) == len(group) for group in HOT)
TOP1, TOP2 = 512, 256
M1, M2 = TOP1 // P, TOP2 // P
X0ROWS = FIELDS + DIM

ZR = 4
PZR = 2

JOBS = ("L1a", "L0b", "L2a", "L1b", "L0c", "L2b")
POOL_UNITS = {"L1a": 2, "L2a": 2, "L1b": 2, "L2b": 2}
POOL_UNITS_LAST = {"L1a": 3, "L2a": 2, "L1b": 2, "L2b": 2}
POOL_AT = {0: (), 1: (5,), 2: (4, 7), 3: (3, 5, 7)}
GATHERS = {"L1a": 10, "L2a": 5, "L1b": 10, "L2b": 7}
GRANULES = {1: (0, 1, 2, 3), 2: (2, 3, 0, 1)}


def layer(job):
    return int(job[1])


class Counts:

    def __init__(self, last):
        self.last = last
        self.jobs = [j for j in JOBS if not (last and j == "L0c")]
        self.share = POOL_UNITS_LAST if last else POOL_UNITS
        self.dve, self.pool, self.mm, at, pat, mat = {}, {}, {}, 0, 0, 0
        self.dve_ends, self.pool_ends = [], []
        for j in self.jobs:
            self.dve[j], self.pool[j] = at, pat
            self.mm[j] = mat
            if layer(j) == 0:
                self.dve_ends += [mat + n + 1 for n in range(L0U)]
                mat += L0U + 1
            else:
                for pos in range(UPJ):
                    (self.pool_ends if pos in POOL_AT[self.share[j]] else self.dve_ends).append(mat + pos + 1)
                mat += UPJ
            at += L0U if layer(j) == 0 else UPJ - self.share[j]
            pat += self.share.get(j, 0)
        self.dve_units, self.pool_units, self.mm_units = at, pat, mat

    def pool_at(self, job):
        return POOL_AT[self.share[job]]

    def units(self, job):
        n = {True: 0, False: 0}
        for pos in range(UPJ):
            on_pool = pos in self.pool_at(job)
            yield pos, GRANULES[layer(job)][pos // 2], pos % 2, on_pool, n[on_pool]
            n[on_pool] += 1

    def job_number(self, job, i):
        return 6 * i + 2 + self.jobs.index(job)

    def dve_before(self, job, i):
        return L0U + i * BODY.dve_units + self.dve[job]

    def pool_before(self, job, i):
        return i * BODY.pool_units + self.pool[job]

    def used(self, job, i, granule):
        return self.mm_before(job, i) + 2 * GRANULES[layer(job)].index(granule) + 2

    def job_end(self, job, i):
        n = L0U if layer(job) == 0 else UPJ - self.share[job]
        return self.dve_before(job, i) + n, self.pool_before(job, i) + self.share.get(job, 0)

    def mm_before(self, job, i):
        return L0U + 1 + i * BODY.mm_units + self.mm[job]

    def mm_end(self, job, i):
        return self.mm_before(job, i) + (L0U + 1 if layer(job) == 0 else UPJ)

    def mm_when_free(self, job, n, on_pool, i):
        mine, before, ring = (self.pool_ends, BODY.pool_ends, PZR) if on_pool else (self.dve_ends, BODY.dve_ends, ZR)
        u = (self.pool if on_pool else self.dve)[job] + n - ring
        off = mine[u] if u >= 0 else max(before[u] - BODY.mm_units, -L0U)
        return L0U + 1 + i * BODY.mm_units + off


BODY, LAST = Counts(False), Counts(True)
assert BODY.dve_units % ZR == 0 and BODY.pool_units % PZR == 0
assert sum(GATHERS.values()) == FIELDS


def pair_of(job, i):
    return 2 * i + "abc".index(job[2])


def program(nc, dense_ctx, ids, tables, w_top1, b_top1, w_top2, b_top2, w_top3, w0, w1, w2, out):
    ctx = ExitStack()
    with ctx:
        def sb(name, shape, dt=F32):
            return ctx.enter_context(nc.sbuf_tensor(name, shape, dt))

        def sem(name):
            return ctx.enter_context(nc.semaphore(name))

        x0_dram = nc.dram_tensor("x0_dram", (TILES, X0ROWS, TCOLS), F32)
        w0_h2 = nc.dram_tensor("w0_h2", (FIELDS, 2 * FIELDS, HID), F32)
        w0_m2 = nc.dram_tensor("w0_m2", (X0ROWS, FIELDS, HID), F32)

        idx = sb("idx", [P, FIELDS], I32)
        idx1 = sb("idx1", [P, FIELDS], I32)
        emb = sb("emb", [P, FIELDS * DIM])
        dctx = sb("dctx", [P, DENSE])
        ident = sb("ident", [P, P])
        x0t = sb("x0t", [P, 4, P])
        rep = sb("rep", [P, PC])
        shf = sb("shf", [P, 4, PC])
        bc = sb("bc", [P, 6, GR, PC])
        z = sb("z", [P, ZR, UNIT, PC])
        pz = sb("pz", [P, PZR, UNIT, PC])
        z16 = sb("z16", [P, PC])
        xdup = sb("xdup", [P, 2, PC])
        xs = sb("xs", [P, 2, CH])
        zp = sb("zp", [P, 3, 2, P])
        zin = sb("zin", [P, 3, P])
        dense_t = sb("dense_t", [DENSE, P])
        h1 = sb("h1", [P, M1, P])
        h2 = sb("h2", [P, M2, P])
        yrow = sb("yrow", [1, P])
        w0s = sb("w0s", [P, 4, HID])
        w16s = sb("w16s", [P, HID])
        w0a = pz[:, 1, 0, 0:4 * HID].rearrange("p (t k) -> p t k", k=HID)
        w0b = pz[:, 1, 0, 4 * HID:8 * HID].rearrange("p (t k) -> p t k", k=HID)
        w16a = pz[0:DIM, 1, 0, 8 * HID:9 * HID]
        w16b = pz[0:DIM, 1, 0, 9 * HID:10 * HID]
        bc_flat = bc.rearrange("p s t c -> p (s t c)")
        used = 0

        def borrow(words):
            nonlocal used
            used += words
            assert used <= 6 * GR * PC
            return bc_flat[0:HP, used - words:used]

        ids_bc = borrow(P * FIELDS).bitcast(I32).rearrange("p (b t) -> p b t", t=FIELDS)
        row_no = borrow(2 * HOT_C).bitcast(I32).rearrange("p (k c) -> p k c", k=2)
        hot_c = {t: tables[t].shape[0] // HP for t in HOT_TABLES}
        assert all(tables[t].shape[0] == HP * c and c <= HOT_C for t, c in hot_c.items())
        hot_sizes = sorted(set(hot_c.values()))
        assert len(hot_sizes) <= 2
        hot_rows = {t: borrow(c * DIM).rearrange("p (c d) -> p c d", d=DIM) for t, c in hot_c.items()}
        odd_words = sum(c for t, c in hot_c.items() if t % 2) * 2 * DIM
        hot_odd = borrow(odd_words).rearrange("p (c d) -> p c d", d=2 * DIM)
        odd_at = {}
        for t in HOT_TABLES:
            if t % 2:
                odd_at[t] = sum(hot_c[u] for u in odd_at)
        onehot = {t: borrow(c * P).rearrange("p (c b) -> p c b", b=P) for t, c in hot_c.items()}
        wl = sb("wl", [P, 2, KT, HID])
        wt1 = sb("wt1", [P, 3, TOP1])
        wt1d = sb("wt1d", [DENSE, TOP1])
        wt2 = sb("wt2", [P, M1, TOP2])
        wt3 = sb("wt3", [P, M2])
        bt1 = sb("bt1", [P, M1])
        bt2 = sb("bt2", [P, M2])

        y_ps = ctx.enter_context(nc.psum_tensor("y_ps", [P, 2, CH], F32))
        x_ps = ctx.enter_context(nc.psum_tensor("x_ps", [P, 2, PC], F32))
        t_ps = ctx.enter_context(nc.psum_tensor("t_ps", [P, 4, P], F32))
        m_ps = ctx.enter_context(nc.psum_tensor("m_ps", [P, 4, P], F32))

        hot_ps = [m_ps[:, :, :], y_ps[:, 1, :].rearrange("p (q b) -> p q b", b=P)]

        ids_loaded = sem("ids_loaded")
        ids1_loaded = sem("ids1_loaded")
        dctx_loaded = sem("dctx_loaded")
        ids_spread = sem("ids_spread")
        hot_loaded = [sem(f"hot_loaded{n}") for n in range(len(HOT))]
        hot_zeroed = sem("hot_zeroed")
        numbered = sem("numbered")
        onehot_made = sem("onehot_made")
        hot_mm = sem("hot_mm")
        hot_shifted = sem("hot_shifted")
        hot_summed = sem("hot_summed")
        gathered = sem("gathered")
        x0_transposed = sem("x0_transposed")
        x0t_ready = sem("x0t_ready")
        x0_stored = sem("x0_stored")
        l0_loaded = [sem(f"l0_loaded{n}") for n in range(L0U)]
        bc_loaded = [sem(f"bc_loaded{n}") for n in range(6)]
        z_made = sem("z_made")
        z16_made = sem("z16_made")
        pz_made = sem("pz_made")
        x_ready = sem("x_ready")
        xdup_ready = sem("xdup_ready")
        xs_ready = sem("xs_ready")
        dsum_done = sem("dsum_done")
        zin_ready = sem("zin_ready")
        h1_mm = sem("h1_mm")
        h1_ready = sem("h1_ready")
        h2_mm = sem("h2_mm")
        h2_ready = sem("h2_ready")
        y_mm = sem("y_mm")
        contracted = sem("contracted")
        y_copied = sem("y_copied")
        y_stored = sem("y_stored")
        dense_transposed = sem("dense_transposed")
        dense_ready = sem("dense_ready")
        zeroed = sem("zeroed")
        ident_ready = sem("ident_ready")
        w0_copied = sem("w0_copied")
        w0_loaded = sem("w0_loaded")
        w0_summed = sem("w0_summed")
        w_loaded = sem("w_loaded")
        wt_loaded = sem("wt_loaded")

        def bc_slot(pair_parity, granule):
            return granule + (4 * pair_parity if granule < 2 else 0)

        def bc_count(job, i, granule):
            second = "abc".index(job[2])
            return 32 * (i + 1) if granule < 2 else 32 * (2 * i + second + 1)

        def parity(job):
            return "abc".index(job[2]) % 2

        zero_list = [zp[:], zin[:], z16[:], w16s[:]]

        block = ctx.enter_context(nc.Block())

        @block.sync
        def _(sp):
            def load_l0(base):
                for n in range(L0U):
                    for j in range(4):
                        rows = slice(FIELDS * j, FIELDS * (j + 1))
                        if n == 0:
                            sp.dma_start(rep[rows, :], bass.AP(x0_dram, base, [[TCOLS, FIELDS], [1, PC]])).then_inc(l0_loaded[n], 16)
                        first = (4 * UNIT * n + j) * TCOLS
                        sp.dma_start(shf[rows, UNIT * n:UNIT * (n + 1), :],
                                     bass.AP(x0_dram, base + first, [[TCOLS, FIELDS], [4 * TCOLS, UNIT], [1, PC]])).then_inc(l0_loaded[n], 16)
                sp.dma_start(z16[0:DIM, :], bass.AP(x0_dram, base + DIM * TCOLS, [[TCOLS, DIM], [1, PC]])).then_inc(l0_loaded[L0U - 1], 16)

            def load_bc(base, half, granule):
                slot = bc_slot(half, granule)
                for j in range(2):
                    sp.dma_start(bc[HID * j:HID * (j + 1), slot, :, :],
                                 bass.AP(x0_dram, base + j * TCOLS if j else base, [[0, HID], [2 * TCOLS, GR], [1, PC]])).then_inc(bc_loaded[slot], 16)

            def start(tile, half, granule=0):
                return tile * (X0ROWS * TCOLS) + (half * PC + 2 * GR * granule * TCOLS)

            sp.dma_start(idx[:, :], ids[0:P, :]).then_inc(ids_loaded, 16)
            sp.dma_start(ids_bc, bass.AP(ids.tensor, 0, [[0, HP], [FIELDS, P], [1, FIELDS]])).then_inc(ids_spread, 16)
            for n, group in enumerate(HOT):
                for t in group:
                    sp.dma_start(hot_rows[t], tables[t].rearrange("(p c) d -> p c d", p=HP)).then_inc(hot_loaded[n], 16)
            sp.dma_start(idx1[:, :], ids[P:2 * P, :]).then_inc(ids1_loaded, 16)
            sp.dma_start(w0_h2[:, 0:FIELDS, :], w0).then_inc(w0_copied, 16)
            sp.dma_start(w0_h2[:, FIELDS:2 * FIELDS, :], w0).then_inc(w0_copied, 16)
            sp.dma_start(w0_m2[0:FIELDS, :, :], w0).then_inc(w0_copied, 16)
            sp.dma_start(w0_m2[FIELDS:X0ROWS, :, :], w0[0:DIM, :, :]).then_inc(w0_copied, 16)
            for n, w in enumerate((w1, w2)):
                for j in range(2):
                    sp.dma_start(wl[HID * j:HID * (j + 1), n, :, :],
                                 w.rearrange("(t j) h k -> j h t k", j=2)[j]).then_inc(w_loaded, 16)
            sp.wait_ge(w0_copied, 4 * 16)
            for j in range(4):
                rows = slice(FIELDS * j, FIELDS * (j + 1))
                sp.dma_start(w0a[rows, :, :], bass.AP(w0_h2, j * HID, [[(2 * FIELDS + 1) * HID, FIELDS], [4 * HID, 4], [1, HID]])).then_inc(w0_loaded, 16)
                sp.dma_start(w0b[rows, :, :], bass.AP(w0_m2, j * FIELDS * HID, [[(FIELDS + 1) * HID, FIELDS], [4 * FIELDS * HID, 4], [1, HID]])).then_inc(w0_loaded, 16)
            sp.dma_start(w16a, bass.AP(w0_h2, DIM * HID, [[(2 * FIELDS + 1) * HID, DIM], [1, HID]])).then_inc(w0_loaded, 16)
            sp.dma_start(w16b, bass.AP(w0_m2, DIM * FIELDS * HID, [[(FIELDS + 1) * HID, DIM], [1, HID]])).then_inc(w0_loaded, 16)
            for c in range(2):
                sp.dma_start(wt1[HID * c:HID * (c + 1), :, :], w_top1[0:3 * HID, :].rearrange("(l k) n -> k l n", l=3)).then_inc(wt_loaded, 16)
            sp.dma_start(wt1d[:, :], w_top1[3 * HID:3 * HID + DENSE, :]).then_inc(wt_loaded, 16)
            sp.dma_start(wt2[:, :, :], w_top2.rearrange("(t p) n -> p t n", p=P)).then_inc(wt_loaded, 16)
            with nc.allow_non_contiguous_dma(reason="a few hundred words, once"):
                sp.dma_start(wt3[:, :], w_top3.rearrange("(t p) o -> p (t o)", p=P)).then_inc(wt_loaded, 16)
                sp.dma_start(bt1[:, :], b_top1.rearrange("(t p) -> p t", p=P)).then_inc(wt_loaded, 16)
                sp.dma_start(bt2[:, :], b_top2.rearrange("(t p) -> p t", p=P)).then_inc(wt_loaded, 16)
            sp.wait_ge(x0_stored, 2 * 16)
            sp.wait_ge(zeroed, 1 + len(zero_list))
            load_l0(start(0, 0))
            for g in range(4):
                load_bc(start(0, 0, g), 0, g)

            def body(i, c):
                if not c.last:
                    sp.wait_ge(gathered, 16 * (len(COLD) + FIELDS * (i + 1)))
                    sp.dma_start(idx[:, :], ids[bass.ds((i + 2) % TILES * P, P), :]).then_inc(ids_loaded, 16)
                sp.wait_ge(contracted, c.mm_before("L1a", i))
                sp.dma_start(dctx[:, :], dense_ctx[bass.ds(i * P, P), :]).then_inc(dctx_loaded, 16)
                load_l0(start(i, 1))
                load_bc(start(i, 1, 0), 1, 0)
                load_bc(start(i, 1, 1), 1, 1)
                for g in (2, 3):
                    sp.wait_ge(contracted, c.used("L2a", i, g))
                    load_bc(start(i, 1, g), 1, g)
                if c.last:
                    return
                sp.wait_ge(x0_stored, 2 * 16 * (i + 2))
                load_l0(start(i + 1, 0))
                sp.wait_ge(contracted, c.mm_end("L2a", i))
                load_bc(start(i + 1, 0, 0), 0, 0)
                load_bc(start(i + 1, 0, 1), 0, 1)
                for g in (2, 3):
                    sp.wait_ge(contracted, c.used("L2b", i, g))
                    load_bc(start(i + 1, 0, g), 0, g)

            with sp.Fori(0, TILES - 1) as i:
                body(i, BODY)
            body(TILES - 1, LAST)
            sp.wait_ge(y_stored, 16 * (TILES + 1))

        @block.gpsimd
        def _(pool):
            pool.memset(ident[:, :], 0.0).then_inc(zeroed, 1)
            for t in zero_list:
                pool.memset(t, 0.0).then_inc(zeroed, 1)
            pool.memset(xs[:, 1, :], 0.0).then_inc(xs_ready, 1)
            pool.memset(dense_t[:, :], 0.0).then_inc(dense_ready, 1)
            pool.wait_ge(zeroed, 1)
            pool.affine_select(out=ident[:, :], in_=ident[:, :], compare_op=ALU.not_equal, fill=1.0,
                               base=0, pattern=[[-1, P]], channel_multiplier=1).then_inc(ident_ready, 1)

            for k, c in enumerate(hot_sizes):
                pool.iota(row_no[:, k, 0:c], pattern=[[1, c]], base=0, channel_multiplier=c).then_inc(numbered, 1)

            def gather(ts, idx=idx):
                for t in ts:
                    pool.indirect_dma_start(out=emb[:, DIM * t:DIM * (t + 1)], out_offset=None, in_=tables[t],
                                            in_offset=bass.IndirectOffsetOnAxis(ap=idx[:, t:t + 1], axis=0)).then_inc(gathered, 16)

            pool.wait_ge(hot_zeroed, 1)
            pool.wait_ge(ids_loaded, 16)
            gather(COLD)
            pool.wait_ge(ids1_loaded, 16)
            pool.wait_ge(x0_transposed, 1)
            gather(range(FIELDS), idx1)

            def body(i, c):
                got = 0
                for job in ("L1a", "L2a", "L1b", "L2b"):
                    src = layer(job) - 1
                    if c.share[job]:
                        pool.wait_ge(xdup_ready, 2 * pair_of(job, i) + src + 1)
                    for _, g, half, on_pool, n in c.units(job):
                        if not on_pool:
                            continue
                        slot = (c.pool[job] + n) % PZR
                        bslot = bc_slot(parity(job), g)
                        if job == "L1a" and n == 1 and not c.last:
                            pool.wait_ge(ids_loaded, 16 * (i + 2))
                            pool.wait_ge(x0_transposed, i + 2)
                        pool.wait_ge(bc_loaded[bslot], bc_count(job, i, g))
                        pool.wait_ge(contracted, c.mm_when_free(job, n, True, i))
                        pool.tensor_tensor(out=pz[:, slot, :, :],
                                           in0=xdup[:, src, None, :].broadcast_to([P, UNIT, PC]),
                                           in1=bc[:, bslot, UNIT * half:UNIT * (half + 1), :], op=ALU.mult).then_inc(pz_made, 1)
                    if not c.last:
                        with pool.If(i < TILES - 2):
                            gather(range(got, got + GATHERS[job]))
                        got += GATHERS[job]

            with pool.Fori(0, TILES - 1) as i:
                body(i, BODY)
            body(TILES - 1, LAST)

        @block.vector
        def _(dve):
            def l0_units(p, slot0, free):
                for n in range(L0U):
                    dve.wait_ge(l0_loaded[n], (8, 5)[n] * 16 * (p + 1))
                    if free:
                        dve.wait_ge(contracted, free[n])
                    dve.tensor_tensor(out=z[:, (slot0 + n) % ZR, :, :], in0=rep[:, None, :].broadcast_to([P, UNIT, PC]),
                                      in1=shf[:, UNIT * n:UNIT * (n + 1), :], op=ALU.mult).then_inc(z_made, 1)
                dve.tensor_tensor(out=z16[0:DIM, :], in0=rep[0:DIM, :], in1=z16[0:DIM, :], op=ALU.mult).then_inc(z16_made, 1)

            def dsum(number, par, lay, pr):
                dve.wait_ge(xs_ready, number + 1)
                dve.tensor_reduce(out=zp[:, lay, pr, :], in_=xs[:, par, :].rearrange("p (d b) -> p b d", b=P),
                                  op=ALU.add, axis=AX.X).then_inc(dsum_done, 1)

            def zadd(lay, number, mlps):
                dve.wait_ge(dsum_done, number + 1)
                if mlps is not None:
                    dve.wait_ge(h1_mm, mlps)
                dve.tensor_tensor(out=zin[:, lay, :], in0=zp[:, lay, 0, :], in1=zp[:, lay, 1, :], op=ALU.add).then_inc(zin_ready, 1)

            for area in (emb[:, :], hot_odd, hot_ps[0], hot_ps[1]):
                dve.memset(area, 0.0).then_inc(hot_zeroed, 1)
            dve.wait_ge(numbered, len(hot_sizes))
            dve.wait_ge(ids_spread, 16)
            for t in HOT_TABLES:
                k, c = hot_sizes.index(hot_c[t]), hot_c[t]
                dve.tensor_tensor(out=onehot[t], in0=ids_bc[:, None, :, t].broadcast_to([HP, c, P]),
                                  in1=row_no[:, k, 0:c, None].broadcast_to([HP, c, P]), op=ALU.is_equal).then_inc(onehot_made, 1)
            dve.wait_ge(zeroed, 1 + len(zero_list))
            dve.wait_ge(w0_loaded, 10 * 16)
            dve.tensor_copy(w0s[0:FIELDS, 0, :], w0a[0:FIELDS, 0, :]).then_inc(w0_summed, 1)
            dve.tensor_tensor(out=w0s[0:FIELDS, 1:4, :], in0=w0a[0:FIELDS, 1:4, :], in1=w0b[0:FIELDS, 1:4, :], op=ALU.add).then_inc(w0_summed, 1)
            for j in range(1, 4):
                rows = slice(FIELDS * j, FIELDS * (j + 1))
                dve.tensor_tensor(out=w0s[rows, :, :], in0=w0a[rows, :, :], in1=w0b[rows, :, :], op=ALU.add).then_inc(w0_summed, 1)
            dve.tensor_tensor(out=w16s[0:DIM, :], in0=w16a, in1=w16b, op=ALU.add).then_inc(w0_summed, 1)
            dve.wait_ge(hot_mm, len(HOT))
            dve.tensor_copy(x0t[:, :, :], hot_ps[0]).then_inc(hot_summed, 1)
            dve.wait_ge(hot_summed, 1)
            dve.tensor_tensor(out=x0t[:, :, :], in0=x0t[:, :, :], in1=hot_ps[1], op=ALU.add).then_inc(hot_summed, 1)
            dve.wait_ge(hot_summed, 2)
            dve.wait_ge(x0_transposed, 1)
            dve.tensor_tensor(out=x0t[:, :, :], in0=x0t[:, :, :], in1=t_ps[:, :, :], op=ALU.add).then_inc(x0t_ready, 1)
            l0_units(0, 0, None)
            dsum(1, 0, 0, 0)

            def body(i, c):
                def units(job, hooks):
                    if layer(job) == 0:
                        l0_units(pair_of(job, i), L0U + c.dve[job], [c.mm_when_free(job, n, False, i) for n in range(L0U)])
                        return
                    src = layer(job) - 1
                    dve.wait_ge(x_ready, 2 * pair_of(job, i) + src + 1)
                    for _, g, half, on_pool, n in c.units(job):
                        if on_pool:
                            continue
                        if n in hooks:
                            hooks[n]()
                        bslot = bc_slot(parity(job), g)
                        dve.wait_ge(bc_loaded[bslot], bc_count(job, i, g))
                        dve.wait_ge(contracted, c.mm_when_free(job, n, False, i))
                        dve.tensor_tensor(out=z[:, (L0U + c.dve[job] + n) % ZR, :, :],
                                          in0=x_ps[:, src, None, :].broadcast_to([P, UNIT, PC]),
                                          in1=bc[:, bslot, UNIT * half:UNIT * (half + 1), :], op=ALU.mult).then_inc(z_made, 1)

                def sums(job, lay, pr, mlps=None):
                    def run():
                        number = c.job_number(job, i)
                        dsum(number, c.jobs.index(job) % 2, lay, pr)
                        if mlps is not None:
                            zadd(lay, number, mlps)
                    return run

                def sums_before():
                    dsum(6 * i + 1, 1, 2, 1)
                    zadd(2, 6 * i + 1, None)

                units("L1a", {3: sums_before})
                units("L0b", {})
                units("L2a", {2: sums("L1a", 1, 0), 5: sums("L0b", 0, 1, i + 1)})
                units("L1b", {3: sums("L2a", 2, 0)})
                if not c.last:
                    units("L0c", {})
                    units("L2b", {2: sums("L1b", 1, 1, i + 1), 5: sums("L0c", 0, 0)})
                else:
                    units("L2b", {3: sums("L1b", 1, 1, i + 1)})
                    sums("L2b", 2, 1, i + 1)()

            with dve.Fori(0, TILES - 1) as i:
                body(i, BODY)
            body(TILES - 1, LAST)

        @block.scalar
        def _(act):
            def spread(bank, src, psum_first=True):
                both = [(x_ps, x_ready), (xdup, xdup_ready)]
                for dst, done in both if psum_first else both[::-1]:
                    for c in range(2):
                        for half in range(2):
                            op = act.activation(dst[HID * half:HID * (half + 1), src, CH * c:CH * (c + 1)],
                                                y_ps[HID * c:HID * (c + 1), bank, :], ACT.Relu)
                    op.then_inc(done, 1)

            def keep(bank, par):
                act.activation(xs[:, par, :], y_ps[:, bank, :], ACT.Relu).then_inc(xs_ready, 1)

            def copy_x0(tile):
                act.wait_ge(x0_transposed, tile + 1)
                act.activation(x0t[:, :, :], t_ps[:, :, :], ACT.Copy).then_inc(x0t_ready, 1)

            def store_x0(tile):
                act.wait_ge(x0t_ready, tile + 1)
                for row, quarters in ((0, 4), (FIELDS, 2)):
                    dst = bass.AP(x0_dram, tile * (X0ROWS * TCOLS) + row * TCOLS, [[P, P], [8 * TCOLS, quarters], [1, P]])
                    act.dma_start(dst, x0t[:, 0:quarters, :]).then_inc(x0_stored, 16)

            def evac(i, c, job):
                number = c.job_number(job, i)
                par = c.jobs.index(job) % 2
                act.wait_ge(contracted, c.mm_end(job, i))
                if layer(job) < 2:
                    spread(par, layer(job))
                act.wait_ge(dsum_done, number - 1)
                keep(par, par)

            def top1(n):
                act.wait_ge(h1_mm, n + 1)
                for m in range(M1):
                    op = act.activation(h1[:, m, :], m_ps[:, m, :], ACT.Relu, bias=bt1[:, m:m + 1])
                op.then_inc(h1_ready, 1)

            def top2(n):
                act.wait_ge(h2_mm, n + 1)
                for m in range(M2):
                    op = act.activation(h2[:, m, :], m_ps[:, m, :], ACT.Relu, bias=bt2[:, m:m + 1])
                op.then_inc(h2_ready, 1)

            def top3(n, block_row):
                act.wait_ge(y_mm, n + 1)
                act.activation(yrow[:, :], m_ps[0:1, 0, :], ACT.Copy).then_inc(y_copied, 1)
                act.wait_ge(y_copied, n + 1)
                act.dma_start(out[bass.ds(block_row * P, P), :].rearrange("b o -> o b"), yrow[:, :]).then_inc(y_stored, 16)

            act.wait_ge(hot_zeroed, 2)
            for n, group in enumerate(HOT):
                act.wait_ge(hot_loaded[n], 16 * len(group))
                for t in group:
                    if t % 2:
                        act.activation(hot_odd[:, odd_at[t]:odd_at[t] + hot_c[t], DIM:2 * DIM], hot_rows[t], ACT.Copy).then_inc(hot_shifted, 1)
            store_x0(0)
            act.wait_ge(zeroed, 1 + len(zero_list))
            act.wait_ge(wt_loaded, 7 * 16)
            act.wait_ge(contracted, L0U + 1)
            keep(0, 0)
            spread(0, 0, psum_first=False)

            def body(i, c):
                if not c.last:
                    act.wait_ge(x0_stored, 2 * 16 * (i + 1))
                    copy_x0(i + 1)
                    store_x0(i + 1)
                evac(i, c, "L1a")
                top1(i)
                evac(i, c, "L0b")
                top2(i)
                evac(i, c, "L2a")
                top3(i, (i + TILES - 1) % TILES)
                act.wait_ge(dense_transposed, i + 1)
                act.wait_ge(h1_mm, i + 1)
                act.activation(dense_t[:, :], m_ps[0:DENSE, 1, :], ACT.Copy).then_inc(dense_ready, 1)
                evac(i, c, "L1b")
                if not c.last:
                    evac(i, c, "L0c")
                evac(i, c, "L2b")
                act.wait_ge(y_stored, 16 * (i + 1))

            with act.Fori(0, TILES - 1) as i:
                body(i, BODY)
            body(TILES - 1, LAST)
            top1(TILES)
            top2(TILES)
            top3(TILES, TILES - 1)

        @block.tensor
        def _(pe):
            def tile_mms(bank, weights, products, start, stop):
                for c in range(2):
                    op = pe.matmul(y_ps[HID * c:HID * (c + 1), bank, :], weights, products[:, CH * c:CH * (c + 1)],
                                   start=start, stop=stop)
                return op

            def l0_job(first, p, slot0, bank):
                for n in range(L0U):
                    pe.wait_ge(z_made, first + n + 1)
                    for t in range(UNIT):
                        op = tile_mms(bank, w0s[:, UNIT * n + t, :], z[:, (slot0 + n) % ZR, t, :], n == 0 and t == 0, False)
                    op.then_inc(contracted, 1)
                pe.wait_ge(z16_made, p + 1)
                tile_mms(bank, w16s[:, :], z16[:, :], False, True).then_inc(contracted, 1)

            def transposes(tile):
                pe.wait_ge(gathered, 16 * (len(COLD) + FIELDS * tile))
                pe.wait_ge(x0t_ready, tile)
                for q in range(4):
                    op = pe.transpose(t_ps[:, q, :], emb[:, P * q:P * (q + 1)], ident[:, :])
                op.then_inc(x0_transposed, 1)

            pe.wait_ge(hot_zeroed, 4)
            done = odd = 0
            for n, group in enumerate(HOT):
                done += len(group)
                odd += sum(t % 2 for t in group)
                pe.wait_ge(hot_loaded[n], 16 * len(group))
                if odd:
                    pe.wait_ge(hot_shifted, odd)
                pe.wait_ge(onehot_made, done)
                for c in range(HOT_C):
                    for t in group:
                        if c < hot_c[t]:
                            row, q, upper = hot_place(t)
                            rows = hot_odd[:, odd_at[t] + c, :] if upper else hot_rows[t][:, c, :]
                            width = 2 * DIM if upper else DIM
                            op = pe.matmul(hot_ps[upper][row:row + width, q, :], rows, onehot[t][:, c, :], start=c == 0, stop=c == hot_c[t] - 1)
                op.then_inc(hot_mm, 1)
            pe.wait_ge(ident_ready, 1)
            pe.wait_ge(zeroed, 1 + len(zero_list))
            transposes(0)
            pe.wait_ge(w0_summed, 6)
            pe.wait_ge(w_loaded, 4 * 16)
            l0_job(0, 0, 0, 0)
            pe.wait_ge(wt_loaded, 7 * 16)

            def mlp1_begin(n):
                pe.wait_ge(zin_ready, 3 * n)
                pe.wait_ge(dense_ready, n + 1)
                for m in range(M1):
                    cols = slice(P * m, P * (m + 1))
                    pe.matmul(m_ps[:, m, :], wt1d[:, cols], dense_t[:, :], start=m == 0, stop=False, skip_group_check=True)
                    for lay in range(2):
                        pe.matmul(m_ps[:, m, :], wt1[:, lay, cols], zin[:, lay, :], start=False, stop=False, skip_group_check=True)

            def mlp1_end(n):
                pe.wait_ge(zin_ready, 3 * n + 1)
                for m in range(M1):
                    op = pe.matmul(m_ps[:, m, :], wt1[:, 2, P * m:P * (m + 1)], zin[:, 2, :], start=False, stop=True, skip_group_check=True)
                op.then_inc(h1_mm, 1)

            def mlp1(n):
                pe.wait_ge(zin_ready, 3 * n + 1)
                pe.wait_ge(dense_ready, n + 1)
                for m in range(M1):
                    cols = slice(P * m, P * (m + 1))
                    for lay in range(3):
                        pe.matmul(m_ps[:, m, :], wt1[:, lay, cols], zin[:, lay, :], start=lay == 0, stop=False)
                    op = pe.matmul(m_ps[:, m, :], wt1d[:, cols], dense_t[:, :], start=False, stop=True)
                op.then_inc(h1_mm, 1)

            def mlp2(n):
                pe.wait_ge(h1_ready, n + 1)
                for m in range(M2):
                    for t in range(M1):
                        op = pe.matmul(m_ps[:, m, :], wt2[:, t, P * m:P * (m + 1)], h1[:, t, :], start=t == 0, stop=t == M1 - 1)
                op.then_inc(h2_mm, 1)

            def mlp3(n):
                pe.wait_ge(h2_ready, n + 1)
                for t in range(M2):
                    op = pe.matmul(m_ps[0:1, 0, :], wt3[:, t:t + 1], h2[:, t, :], start=t == 0, stop=t == M2 - 1)
                op.then_inc(y_mm, 1)

            def dense(i):
                pe.wait_ge(dctx_loaded, 16 * (i + 1))
                pe.wait_ge(y_copied, i + 1)
                pe.transpose(m_ps[0:DENSE, 1, :], dctx[:, :], ident[:, :]).then_inc(dense_transposed, 1)

            def body(i, c):
                def job(name, middle=None, at=4):
                    number = c.job_number(name, i)
                    bank = c.jobs.index(name) % 2
                    pe.wait_ge(xs_ready, number - 1)
                    if layer(name) == 0:
                        l0_job(c.dve_before(name, i), pair_of(name, i), L0U + c.dve[name], bank)
                        return
                    for pos, g, half, on_pool, n in c.units(name):
                        if pos == at and middle:
                            middle()
                        if on_pool:
                            pe.wait_ge(pz_made, c.pool_before(name, i) + n + 1)
                            src = pz[:, (c.pool[name] + n) % PZR, :, :]
                        else:
                            pe.wait_ge(z_made, c.dve_before(name, i) + n + 1)
                            src = z[:, (L0U + c.dve[name] + n) % ZR, :, :]
                        for t in range(UNIT):
                            op = tile_mms(bank, wl[:, layer(name) - 1, GR * g + UNIT * half + t, :], src[:, t, :],
                                          pos == 0 and t == 0, pos == UPJ - 1 and t == UNIT - 1)
                        op.then_inc(contracted, 1)

                job("L1a", middle=None if c.last else lambda: transposes(i + 1))
                mlp1(i)
                job("L0b")
                mlp2(i)
                job("L2a")
                mlp3(i)
                job("L1b", middle=lambda: dense(i))
                if not c.last:
                    job("L0c")
                job("L2b", middle=(lambda: mlp1_begin(TILES)) if c.last else None, at=UPJ - 1)

            with pe.Fori(0, TILES - 1) as i:
                body(i, BODY)
            body(TILES - 1, LAST)
            mlp1_end(TILES)
            mlp2(TILES)
            mlp3(TILES)


def kernel(**inputs):
    import numpy as np
    import concourse.bacc as bacc
    from concourse.bass_utils import run_bass_kernel_spmd

    nc = bacc.Bacc("TRN2", target_bir_lowering=False, num_devices=1, dynamic_dma_scratch_size=8192)
    arrays, args = {}, {}
    for name, value in inputs.items():
        a = np.ascontiguousarray(value)
        arrays[f"in_{name}"] = a
        args[name] = nc.dram_tensor(f"in_{name}", a.shape, mybir.dt.from_np(a.dtype), kind="ExternalInput").ap()
    out = nc.dram_tensor("out_0", (BATCH, 1), F32, kind="ExternalOutput").ap()
    program(nc, args["dense_ctx"], args["ids"], [args[f"tbl_{t}"] for t in range(FIELDS)],
            args["W_top1"], args["b_top1"], args["W_top2"], args["b_top2"], args["W_top3"],
            args["L0_rec_W0"], args["L0_rec_W1"], args["L0_rec_W2"], out)
    return run_bass_kernel_spmd(nc, [arrays], core_ids=[0]).results[0]["out_0"]
```

```python
from contextlib import ExitStack, nullcontext

import concourse.bass as bass
from concourse import mybir

F32 = mybir.dt.float32
I32 = mybir.dt.int32
ALU = mybir.AluOpType
ACT = mybir.ActivationFunctionType
AX = mybir.AxisListType

BATCH, FIELDS, DIM = 512, 32, 16
HID = 64
P = 128
TILES = BATCH // P
TCOLS = DIM * P
CH = 512
PC = 2 * CH
KT = FIELDS * HID // P
GR = 4
UNIT = 2
UPJ = KT // UNIT
L0U = 2
DENSE = 16
HOT = ((18, 20, 22, 24), (0, 26), (2,), (1,), (25,), (17, 19, 21, 23))
HP, HOT_C = 125, 10
HOT_TABLES = [t for group in HOT for t in group]
COLD = [t for t in range(FIELDS) if t not in HOT_TABLES]


def hot_place(t):
    return 2 * DIM * (t % 8 // 2), t // 8, t % 2


EVEN_GROUPS = sum(group[0] % 2 == 0 for group in HOT)
assert all(t % 2 == (n >= EVEN_GROUPS) for n, group in enumerate(HOT) for t in group)
assert all(len({hot_place(t)[0] for t in group}) == len(group) for group in HOT)
TOP1, TOP2 = 512, 256
M1, M2 = TOP1 // P, TOP2 // P
X0ROWS = FIELDS + DIM

MADE = 2

MLP3_AT = 1
TRANSPOSE_AT = 6

ZR = 4
PZR = 2

JOBS = ("L1a", "L0b", "L2a", "L1b", "L0c", "L2b")
POOL_UNITS = {"L1a": 2, "L2a": 2, "L1b": 2, "L2b": 2}
POOL_UNITS_LAST = {"L1a": 3, "L2a": 2, "L1b": 2, "L2b": 2}
POOL_AT = {0: (), 1: (5,), 2: (3, 6), 3: (3, 5, 7)}
FIRST_L1A = (4, 6)
FIRST = 16
BETWEEN = 3
GATHERS = {"L1a": range(FIRST, FIELDS), "L2a": range(0), "L1b": range(0, 10), "L2b": range(10, FIRST)}
GRANULES = {1: (0, 1, 2, 3), 2: (2, 3, 0, 1)}


def layer(job):
    return int(job[1])


class Counts:

    def __init__(self, first=False, last=False):
        self.first, self.last = first, last
        self.jobs = [j for j in JOBS if not (last and j == "L0c")]
        self.share = POOL_UNITS_LAST if last else POOL_UNITS
        self.dve, self.pool, self.mm, at, pat, mat = {}, {}, {}, 0, 0, 0
        self.dve_ends, self.pool_ends = [], []
        for j in self.jobs:
            self.dve[j], self.pool[j] = at, pat
            self.mm[j] = mat
            if layer(j) == 0:
                self.dve_ends += [mat + n + 1 for n in range(L0U)]
                mat += L0U + 1
            else:
                for pos in range(UPJ):
                    (self.pool_ends if pos in self.pool_at(j) else self.dve_ends).append(mat + pos + 1)
                mat += UPJ
            at += L0U if layer(j) == 0 else UPJ - self.share[j]
            pat += self.share.get(j, 0)
        self.dve_units, self.pool_units, self.mm_units = at, pat, mat

    def pool_at(self, job):
        return FIRST_L1A if self.first and job == "L1a" else POOL_AT[self.share[job]]

    def units(self, job):
        n = {True: 0, False: 0}
        for pos in range(UPJ):
            on_pool = pos in self.pool_at(job)
            yield pos, GRANULES[layer(job)][pos // 2], pos % 2, on_pool, n[on_pool]
            n[on_pool] += 1

    def job_number(self, job, i):
        return len(JOBS) * i + 1 + self.jobs.index(job)

    def dve_before(self, job, i):
        return L0U + i * BODY.dve_units + self.dve[job]

    def pool_before(self, job, i):
        return i * BODY.pool_units + self.pool[job]

    def used(self, job, i, granule):
        return self.mm_before(job, i) + 2 * GRANULES[layer(job)].index(granule) + 2

    def job_end(self, job, i):
        n = L0U if layer(job) == 0 else UPJ - self.share[job]
        return self.dve_before(job, i) + n, self.pool_before(job, i) + self.share.get(job, 0)

    def mm_before(self, job, i):
        return L0U + 1 + i * BODY.mm_units + self.mm[job]

    def mm_end(self, job, i):
        return self.mm_before(job, i) + (L0U + 1 if layer(job) == 0 else UPJ)

    def mm_when_free(self, job, n, on_pool, i):
        mine, before, ring = (self.pool_ends, BODY.pool_ends, PZR) if on_pool else (self.dve_ends, BODY.dve_ends, ZR)
        u = (self.pool if on_pool else self.dve)[job] + n - ring
        off = mine[u] if u >= 0 else max(before[u] - BODY.mm_units, -L0U)
        return L0U + 1 + i * BODY.mm_units + off


BODY, FIRST_BODY, LAST = Counts(), Counts(first=True), Counts(last=True)
assert BODY.dve_units % ZR == 0 and BODY.pool_units % PZR == 0
assert sorted(t for ts in GATHERS.values() for t in ts) == list(range(FIELDS))


def pair_of(job, i):
    return 2 * i + "abc".index(job[2])


def program(nc, dense_ctx, ids, tables, w_top1, b_top1, w_top2, b_top2, w_top3, w0, w1, w2, out):
    ctx = ExitStack()
    with ctx:
        def sb(name, shape, dt=F32):
            return ctx.enter_context(nc.sbuf_tensor(name, shape, dt))

        def sem(name):
            return ctx.enter_context(nc.semaphore(name))

        x0_dram = nc.dram_tensor("x0_dram", (TILES, X0ROWS, TCOLS), F32)
        w0_h2 = nc.dram_tensor("w0_h2", (FIELDS, 2 * FIELDS, HID), F32)
        w0_m2 = nc.dram_tensor("w0_m2", (X0ROWS, FIELDS, HID), F32)

        idx0 = sb("idx0", [P, FIELDS], I32)
        idx = sb("idx", [P, FIELDS], I32)
        emb = sb("emb", [P, FIELDS * DIM])
        dctx = sb("dctx", [P, DENSE])
        ident = sb("ident", [P, P])
        x0t = sb("x0t", [P, 4, P])
        rep = sb("rep", [P, PC])
        shf = sb("shf", [P, 4, PC])
        bc = sb("bc", [P, 6, GR, PC])
        z = sb("z", [P, ZR, UNIT, PC])
        pz = sb("pz", [P, PZR, UNIT, PC])
        z16 = sb("z16", [P, PC])
        xdup = sb("xdup", [P, 2, PC])
        xs = sb("xs", [P, 2, CH])
        zp = sb("zp", [P, 3, 2, P])
        zin = sb("zin", [P, 3, P])
        dense_t = sb("dense_t", [DENSE, P])
        h1 = sb("h1", [P, M1, P])
        h2 = sb("h2", [P, M2, P])
        yrow = sb("yrow", [1, P])
        w0s = sb("w0s", [P, 4, HID])
        w16s = sb("w16s", [P, HID])
        w0a = pz[:, 1, 0, 0:4 * HID].rearrange("p (t k) -> p t k", k=HID)
        w0b = pz[:, 1, 0, 4 * HID:8 * HID].rearrange("p (t k) -> p t k", k=HID)
        w16a = pz[0:DIM, 1, 0, 8 * HID:9 * HID]
        w16b = pz[0:DIM, 1, 0, 9 * HID:10 * HID]
        bc_flat = bc.rearrange("p s t c -> p (s t c)")
        used = 0

        def borrow(words):
            nonlocal used
            used += words
            assert used <= 6 * GR * PC
            return bc_flat[0:HP, used - words:used]

        ids_bc = borrow(P * FIELDS).bitcast(I32).rearrange("p (b t) -> p b t", t=FIELDS)
        row_no = borrow(2 * HOT_C).bitcast(I32).rearrange("p (k c) -> p k c", k=2)
        hot_c = {t: tables[t].shape[0] // HP for t in HOT_TABLES}
        assert all(tables[t].shape[0] == HP * c and c <= HOT_C for t, c in hot_c.items())
        hot_sizes = sorted(set(hot_c.values()))
        assert len(hot_sizes) <= 2
        hot_rows = {t: borrow(c * DIM).rearrange("p (c d) -> p c d", d=DIM) for t, c in hot_c.items()}
        odd_words = sum(c for t, c in hot_c.items() if t % 2) * 2 * DIM
        hot_odd = borrow(odd_words).rearrange("p (c d) -> p c d", d=2 * DIM)
        odd_at = {}
        for t in HOT_TABLES:
            if t % 2:
                odd_at[t] = sum(hot_c[u] for u in odd_at)
        onehot = {t: borrow(c * P).rearrange("p (c b) -> p c b", b=P) for t, c in hot_c.items()}
        used += GR * P
        assert used <= 6 * GR * PC
        pick = bc_flat[:, used - GR * P:used]
        wl = sb("wl", [P, 2, KT, HID])
        wt1 = sb("wt1", [P, 3, TOP1])
        wt1d = sb("wt1d", [DENSE, TOP1])
        wt2 = sb("wt2", [P, M1, TOP2])
        wt3 = sb("wt3", [P, M2])
        bt1 = sb("bt1", [P, M1])
        bt2 = sb("bt2", [P, M2])

        y_ps = ctx.enter_context(nc.psum_tensor("y_ps", [P, 2, CH], F32))
        x_ps = ctx.enter_context(nc.psum_tensor("x_ps", [P, 2, PC], F32))
        t_ps = ctx.enter_context(nc.psum_tensor("t_ps", [P, 4, P], F32))
        m_ps = ctx.enter_context(nc.psum_tensor("m_ps", [P, 4, P], F32))

        hot_ps = [m_ps[:, :, :], y_ps[:, 1, :].rearrange("p (q b) -> p q b", b=P)]

        ids_loaded = sem("ids_loaded")
        ids0_loaded = sem("ids0_loaded")
        ids1_loaded = sem("ids1_loaded")
        dctx_loaded = sem("dctx_loaded")
        ids_spread = sem("ids_spread")
        hot_loaded = [sem(f"hot_loaded{n}") for n in range(len(HOT))]
        hot_zeroed = sem("hot_zeroed")
        numbered = sem("numbered")
        onehot_made = sem("onehot_made")
        hot_mm = sem("hot_mm")
        hot_shifted = sem("hot_shifted")
        hot_copied = sem("hot_copied")
        hot_summed = sem("hot_summed")
        gathered = sem("gathered")
        x0_transposed = sem("x0_transposed")
        x0t_ready = sem("x0t_ready")
        x0_stored = sem("x0_stored")
        l0_loaded = [sem(f"l0_loaded{n}") for n in range(L0U)]
        l0_first = [sem(f"l0_first{t}") for t in range(4)]
        rep_loaded = sem("rep_loaded")
        pick_ready = sem("pick_ready")
        repeated = sem("repeated")
        first_made = sem("first_made")
        bc_loaded = [sem(f"bc_loaded{n}") for n in range(6)]
        z_made = sem("z_made")
        z16_made = sem("z16_made")
        pz_made = sem("pz_made")
        x_ready = sem("x_ready")
        xdup_ready = sem("xdup_ready")
        xs_ready = sem("xs_ready")
        dsum_done = sem("dsum_done")
        zin_ready = sem("zin_ready")
        h1_mm = sem("h1_mm")
        h1_ready = sem("h1_ready")
        h2_mm = sem("h2_mm")
        h2_ready = sem("h2_ready")
        y_mm = sem("y_mm")
        contracted = sem("contracted")
        y_copied = sem("y_copied")
        y_stored = sem("y_stored")
        dense_transposed = sem("dense_transposed")
        dense_ready = sem("dense_ready")
        zeroed = sem("zeroed")
        ident_ready = sem("ident_ready")
        w0_copied = sem("w0_copied")
        w0_loaded = sem("w0_loaded")
        w0_summed = sem("w0_summed")
        w_loaded = sem("w_loaded")
        wt_loaded = sem("wt_loaded")

        def bc_slot(pair_parity, granule):
            return granule + (4 * pair_parity if granule < 2 else 0)

        def bc_count(job, i, granule):
            second = "abc".index(job[2])
            return 32 * (i + 1) if granule < 2 else 32 * (2 * i + second + 1)

        def parity(job):
            return "abc".index(job[2]) % 2

        made_inc = 32 // (2 * GR)

        zero_list = [zp[:], zin[:], z16[:], w16s[:]]

        block = ctx.enter_context(nc.Block())

        @block.sync
        def _(sp):
            def load_l0(base, loaded=[l0_loaded[t // UNIT] for t in range(4)], rep_loaded=l0_loaded[0]):
                sp.dma_start(rep[:, :], bass.AP(x0_dram, base, [[0, 4], [TCOLS, FIELDS], [1, PC]])).then_inc(rep_loaded, 16)
                for t in range(4):
                    if t == UNIT:
                        sp.dma_start(z16[0:DIM, :], bass.AP(x0_dram, base + DIM * TCOLS, [[TCOLS, DIM], [1, PC]])).then_inc(loaded[t], 16)
                    sp.dma_start(shf[:, t, :], bass.AP(x0_dram, base + 4 * t * TCOLS,
                                                       [[TCOLS, 4], [TCOLS, FIELDS], [1, PC]])).then_inc(loaded[t], 16)

            def load_bc(base, half, granule):
                slot = bc_slot(half, granule)
                for j in range(2):
                    sp.dma_start(bc[HID * j:HID * (j + 1), slot, :, :],
                                 bass.AP(x0_dram, base + j * TCOLS if j else base, [[0, HID], [2 * TCOLS, GR], [1, PC]])).then_inc(bc_loaded[slot], 16)

            def start(tile, half, granule=0):
                return tile * (X0ROWS * TCOLS) + (half * PC + 2 * GR * granule * TCOLS)

            sp.dma_start(idx0[:, :], ids[0:P, :]).then_inc(ids0_loaded, 16)
            sp.dma_start(ids_bc, bass.AP(ids.tensor, 0, [[0, HP], [FIELDS, P], [1, FIELDS]])).then_inc(ids_spread, 16)
            for n, group in enumerate(HOT):
                for t in group:
                    sp.dma_start(hot_rows[t], tables[t].rearrange("(p c) d -> p c d", p=HP)).then_inc(hot_loaded[n], 16)
            sp.dma_start(idx[:, :], ids[P:2 * P, :]).then_inc(ids1_loaded, 16)
            sp.dma_start(w0_h2[:, 0:FIELDS, :], w0).then_inc(w0_copied, 16)
            sp.dma_start(w0_h2[:, FIELDS:2 * FIELDS, :], w0).then_inc(w0_copied, 16)
            sp.dma_start(w0_m2[0:FIELDS, :, :], w0).then_inc(w0_copied, 16)
            sp.dma_start(w0_m2[FIELDS:X0ROWS, :, :], w0[0:DIM, :, :]).then_inc(w0_copied, 16)
            for n, w in enumerate((w1, w2)):
                for j in range(2):
                    sp.dma_start(wl[HID * j:HID * (j + 1), n, :, :],
                                 w.rearrange("(t j) h k -> j h t k", j=2)[j]).then_inc(w_loaded, 16)
            sp.wait_ge(w0_copied, 4 * 16)
            for j in range(4):
                rows = slice(FIELDS * j, FIELDS * (j + 1))
                sp.dma_start(w0a[rows, :, :], bass.AP(w0_h2, j * HID, [[(2 * FIELDS + 1) * HID, FIELDS], [4 * HID, 4], [1, HID]])).then_inc(w0_loaded, 16)
                sp.dma_start(w0b[rows, :, :], bass.AP(w0_m2, j * FIELDS * HID, [[(FIELDS + 1) * HID, FIELDS], [4 * FIELDS * HID, 4], [1, HID]])).then_inc(w0_loaded, 16)
            sp.dma_start(w16a, bass.AP(w0_h2, DIM * HID, [[(2 * FIELDS + 1) * HID, DIM], [1, HID]])).then_inc(w0_loaded, 16)
            sp.dma_start(w16b, bass.AP(w0_m2, DIM * FIELDS * HID, [[(FIELDS + 1) * HID, DIM], [1, HID]])).then_inc(w0_loaded, 16)
            for c in range(2):
                sp.dma_start(wt1[HID * c:HID * (c + 1), :, :], w_top1[0:3 * HID, :].rearrange("(l k) n -> k l n", l=3)).then_inc(wt_loaded, 16)
            sp.dma_start(wt1d[:, :], w_top1[3 * HID:3 * HID + DENSE, :]).then_inc(wt_loaded, 16)
            sp.dma_start(wt2[:, :, :], w_top2.rearrange("(t p) n -> p t n", p=P)).then_inc(wt_loaded, 16)
            with nc.allow_non_contiguous_dma(reason="a few hundred words, once"):
                sp.dma_start(wt3[:, :], w_top3.rearrange("(t p) o -> p (t o)", p=P)).then_inc(wt_loaded, 16)
                sp.dma_start(bt1[:, :], b_top1.rearrange("(t p) -> p t", p=P)).then_inc(wt_loaded, 16)
                sp.dma_start(bt2[:, :], b_top2.rearrange("(t p) -> p t", p=P)).then_inc(wt_loaded, 16)
            sp.wait_ge(x0_stored, 2 * 16)
            sp.wait_ge(zeroed, 1 + len(zero_list))
            load_l0(start(0, 0), l0_first, rep_loaded)
            for g in range(4):
                if g != MADE:
                    load_bc(start(0, 0, g), 0, g)
            sp.wait_ge(repeated, 2 * GR)

            def body(i, c):
                sp.wait_ge(contracted, c.mm_before("L1a", i))
                sp.dma_start(dctx[:, :], dense_ctx[bass.ds(i * P, P), :]).then_inc(dctx_loaded, 16)
                load_l0(start(i, 1))
                load_bc(start(i, 1, 0), 1, 0)
                load_bc(start(i, 1, 1), 1, 1)
                if not c.last:
                    sp.wait_ge(gathered, 16 * (len(COLD) + FIELDS * (i + 1)))
                    sp.dma_start(idx[:, :], ids[bass.ds((i + 2) % TILES * P, P), :]).then_inc(ids_loaded, 16)
                for g in (2, 3):
                    sp.wait_ge(contracted, c.used("L2a", i, g))
                    load_bc(start(i, 1, g), 1, g)
                if c.last:
                    return
                sp.wait_ge(x0_stored, 2 * 16 * (i + 2))
                load_l0(start(i + 1, 0))
                sp.wait_ge(contracted, c.mm_end("L2a", i))
                load_bc(start(i + 1, 0, 0), 0, 0)
                load_bc(start(i + 1, 0, 1), 0, 1)
                for g in (2, 3):
                    sp.wait_ge(contracted, c.used("L2b", i, g))
                    load_bc(start(i + 1, 0, g), 0, g)

            body(0, FIRST_BODY)
            with sp.Fori(1, TILES - 1) as i:
                body(i, BODY)
            body(TILES - 1, LAST)
            sp.wait_ge(y_stored, 16 * TILES)

        @block.gpsimd
        def _(pool):
            pool.memset(ident[:, :], 0.0).then_inc(zeroed, 1)
            for t in zero_list:
                pool.memset(t, 0.0).then_inc(zeroed, 1)
            pool.wait_ge(zeroed, 1)
            pool.affine_select(out=ident[:, :], in_=ident[:, :], compare_op=ALU.not_equal, fill=1.0,
                               base=0, pattern=[[-1, P]], channel_multiplier=1).then_inc(ident_ready, 1)

            for k, c in enumerate(hot_sizes):
                pool.iota(row_no[:, k, 0:c], pattern=[[1, c]], base=0, channel_multiplier=c).then_inc(numbered, 1)

            def gather(ts, idx=idx):
                for t in ts:
                    pool.indirect_dma_start(out=emb[:, DIM * t:DIM * (t + 1)], out_offset=None, in_=tables[t],
                                            in_offset=bass.IndirectOffsetOnAxis(ap=idx[:, t:t + 1], axis=0)).then_inc(gathered, 16)

            pool.wait_ge(hot_zeroed, 1)
            pool.wait_ge(ids0_loaded, 16)
            gather(COLD, idx0)
            pool.wait_ge(ids1_loaded, 16)
            pool.wait_ge(x0_transposed, 1)
            gather(range(FIRST))

            def body(i, c):
                for job in ("L1a", "L2a", "L1b", "L2b"):
                    src = layer(job) - 1
                    if c.share[job]:
                        pool.wait_ge(xdup_ready, 2 * pair_of(job, i) + src + 1)
                    for _, g, half, on_pool, n in c.units(job):
                        if not on_pool:
                            continue
                        slot = (c.pool[job] + n) % PZR
                        bslot = bc_slot(parity(job), g)
                        if n == 1 and not c.last:
                            if job == "L1b":
                                pool.wait_ge(ids_loaded, 16 * (i + 1))
                                pool.wait_ge(x0_transposed, i + 2)
                        pool.wait_ge(bc_loaded[bslot], bc_count(job, i, g))
                        pool.wait_ge(contracted, c.mm_when_free(job, n, True, i))
                        pool.tensor_tensor(out=pz[:, slot, :, :],
                                           in0=xdup[:, src, None, :].broadcast_to([P, UNIT, PC]),
                                           in1=bc[:, bslot, UNIT * half:UNIT * (half + 1), :], op=ALU.mult).then_inc(pz_made, 1)
                        if n == 0 and job == "L1a" and not c.last:
                            gather(GATHERS[job][:BETWEEN])
                    if c.last:
                        continue
                    if job[2] == "a":
                        gather(GATHERS[job][BETWEEN if job == "L1a" else 0:])
                    else:
                        with nullcontext() if c.first else pool.If(i < TILES - 2):
                            gather(GATHERS[job])

            body(0, FIRST_BODY)
            with pool.Fori(1, TILES - 1) as i:
                body(i, BODY)
            body(TILES - 1, LAST)

        @block.vector
        def _(dve):
            def l0_units(p, slot0, free):
                for n in range(L0U):
                    dve.wait_ge(l0_loaded[n], 3 * 16 * p)
                    dve.wait_ge(contracted, free[n])
                    dve.tensor_tensor(out=z[:, (slot0 + n) % ZR, :, :], in0=rep[:, None, :].broadcast_to([P, UNIT, PC]),
                                      in1=shf[:, UNIT * n:UNIT * (n + 1), :], op=ALU.mult).then_inc(z_made, 1)
                dve.tensor_tensor(out=z16[0:DIM, :], in0=rep[0:DIM, :], in1=z16[0:DIM, :], op=ALU.mult).then_inc(z16_made, 1)

            def dsum(number, par, lay, pr):
                dve.wait_ge(xs_ready, number + 1)
                dve.tensor_reduce(out=zp[:, lay, pr, :], in_=xs[:, par, :].rearrange("p (d b) -> p b d", b=P),
                                  op=ALU.add, axis=AX.X).then_inc(dsum_done, 1)

            def zadd(lay, number, mlps):
                dve.wait_ge(dsum_done, number + 1)
                if mlps is not None:
                    dve.wait_ge(h1_mm, mlps)
                dve.tensor_tensor(out=zin[:, lay, :], in0=zp[:, lay, 0, :], in1=zp[:, lay, 1, :], op=ALU.add).then_inc(zin_ready, 1)

            for area in (emb[:, :], hot_odd, hot_ps[0], hot_ps[1]):
                dve.memset(area, 0.0).then_inc(hot_zeroed, 1)
            dve.wait_ge(numbered, len(hot_sizes))
            dve.wait_ge(ids_spread, 16)
            for t in HOT_TABLES:
                k, c = hot_sizes.index(hot_c[t]), hot_c[t]
                dve.tensor_tensor(out=onehot[t], in0=ids_bc[:, None, :, t].broadcast_to([HP, c, P]),
                                  in1=row_no[:, k, 0:c, None].broadcast_to([HP, c, P]), op=ALU.is_equal).then_inc(onehot_made, 1)
            dve.wait_ge(zeroed, 1 + len(zero_list))
            dve.wait_ge(w0_loaded, 10 * 16)
            dve.tensor_copy(w0s[0:FIELDS, 0, :], w0a[0:FIELDS, 0, :]).then_inc(w0_summed, 1)
            dve.tensor_tensor(out=w0s[0:FIELDS, 1:4, :], in0=w0a[0:FIELDS, 1:4, :], in1=w0b[0:FIELDS, 1:4, :], op=ALU.add).then_inc(w0_summed, 1)
            for j in range(1, 4):
                rows = slice(FIELDS * j, FIELDS * (j + 1))
                dve.tensor_tensor(out=w0s[rows, :, :], in0=w0a[rows, :, :], in1=w0b[rows, :, :], op=ALU.add).then_inc(w0_summed, 1)
            dve.tensor_tensor(out=w16s[0:DIM, :], in0=w16a, in1=w16b, op=ALU.add).then_inc(w0_summed, 1)
            dve.wait_ge(ident_ready, 1)
            dve.memset(pick, 0.0).then_inc(pick_ready, 1)
            dve.wait_ge(pick_ready, 1)
            dve.tensor_copy(pick[0:FIELDS, :].rearrange("m (r n) -> m r n", n=HID),
                            ident[0:FIELDS, 2 * GR * MADE:2 * GR * (MADE + 1), None].broadcast_to([FIELDS, 2 * GR, HID])).then_inc(pick_ready, 1)
            dve.wait_ge(hot_mm, len(HOT))
            dve.wait_ge(hot_copied, 1)
            dve.tensor_tensor(out=x0t[:, :, :], in0=x0t[:, :, :], in1=hot_ps[1], op=ALU.add).then_inc(hot_summed, 1)
            dve.wait_ge(hot_summed, 1)
            dve.wait_ge(x0_transposed, 1)
            dve.tensor_tensor(out=x0t[:, :, :], in0=x0t[:, :, :], in1=t_ps[:, :, :], op=ALU.add).then_inc(x0t_ready, 1)
            dve.wait_ge(rep_loaded, 16)
            for t in range(4):
                dve.wait_ge(l0_first[t], 16 * (2 if t == UNIT else 1))
                if t == UNIT:
                    dve.tensor_tensor(out=z16[0:DIM, :], in0=rep[0:DIM, :], in1=z16[0:DIM, :], op=ALU.mult).then_inc(z16_made, 1)
                dve.tensor_tensor(out=z[:, t // UNIT, t % UNIT, :], in0=rep[:, :], in1=shf[:, t, :],
                                  op=ALU.mult).then_inc(z_made if t % UNIT else first_made, 1)
            dsum(0, 0, 0, 0)

            def body(i, c):
                def units(job, hooks):
                    if layer(job) == 0:
                        l0_units(pair_of(job, i), L0U + c.dve[job], [c.mm_when_free(job, n, False, i) for n in range(L0U)])
                        return
                    src = layer(job) - 1
                    dve.wait_ge(x_ready, 2 * pair_of(job, i) + src + 1)
                    for _, g, half, on_pool, n in c.units(job):
                        if on_pool:
                            continue
                        if n in hooks:
                            hooks[n]()
                        bslot = bc_slot(parity(job), g)
                        dve.wait_ge(bc_loaded[bslot], bc_count(job, i, g))
                        dve.wait_ge(contracted, c.mm_when_free(job, n, False, i))
                        dve.tensor_tensor(out=z[:, (L0U + c.dve[job] + n) % ZR, :, :],
                                          in0=x_ps[:, src, None, :].broadcast_to([P, UNIT, PC]),
                                          in1=bc[:, bslot, UNIT * half:UNIT * (half + 1), :], op=ALU.mult).then_inc(z_made, 1)

                def sums(job, lay, pr, add=False):
                    def run():
                        number = c.job_number(job, i)
                        dsum(number, c.jobs.index(job) % 2, lay, pr)
                        if add:
                            zadd(lay, number, None if c.first else i)
                    return run

                def sums_before():
                    dsum(len(JOBS) * i, 1, 2, 1)
                    zadd(2, len(JOBS) * i, None)

                units("L1a", {} if c.first else {3: sums_before})
                units("L0b", {})
                units("L2a", {2: sums("L1a", 1, 0), 5: sums("L0b", 0, 1, add=True)})
                units("L1b", {3: sums("L2a", 2, 0)})
                if not c.last:
                    units("L0c", {})
                    units("L2b", {2: sums("L1b", 1, 1, add=True), 5: sums("L0c", 0, 0)})
                else:
                    units("L2b", {3: sums("L1b", 1, 1, add=True)})
                    sums("L2b", 2, 1, add=True)()

            body(0, FIRST_BODY)
            with dve.Fori(1, TILES - 1) as i:
                body(i, BODY)
            body(TILES - 1, LAST)

        @block.scalar
        def _(act):
            def spread(bank, src):
                for dst, done in ((x_ps, x_ready), (xdup, xdup_ready)):
                    for c in range(2):
                        for half in range(2):
                            op = act.activation(dst[HID * half:HID * (half + 1), src, CH * c:CH * (c + 1)],
                                                y_ps[HID * c:HID * (c + 1), bank, :], ACT.Relu)
                    op.then_inc(done, 1)

            def keep(bank, par):
                act.activation(xs[:, par, :], y_ps[:, bank, :], ACT.Relu).then_inc(xs_ready, 1)

            def copy_x0(tile):
                act.wait_ge(x0_transposed, tile + 1)
                act.activation(x0t[:, :, :], t_ps[:, :, :], ACT.Copy).then_inc(x0t_ready, 1)

            def store_x0(tile):
                act.wait_ge(x0t_ready, tile + 1)
                for row, quarters in ((0, 4), (FIELDS, 2)):
                    dst = bass.AP(x0_dram, tile * (X0ROWS * TCOLS) + row * TCOLS, [[P, P], [8 * TCOLS, quarters], [1, P]])
                    act.dma_start(dst, x0t[:, 0:quarters, :]).then_inc(x0_stored, 16)

            def evac(i, c, job):
                number = c.job_number(job, i)
                par = c.jobs.index(job) % 2
                act.wait_ge(contracted, c.mm_end(job, i))
                if layer(job) < 2:
                    spread(par, layer(job))
                act.wait_ge(dsum_done, max(number - 1, 1) if c.first else number - 1)
                keep(par, par)

            def top1(n):
                act.wait_ge(h1_mm, n)
                for m in range(M1):
                    op = act.activation(h1[:, m, :], m_ps[:, m, :], ACT.Relu, bias=bt1[:, m:m + 1])
                op.then_inc(h1_ready, 1)

            def top2(n):
                act.wait_ge(h2_mm, n)
                for m in range(M2):
                    op = act.activation(h2[:, m, :], m_ps[:, m, :], ACT.Relu, bias=bt2[:, m:m + 1])
                op.then_inc(h2_ready, 1)

            def top3(n, block_row):
                act.wait_ge(y_mm, n)
                act.activation(yrow[:, :], m_ps[0:1, 0, :], ACT.Copy).then_inc(y_copied, 1)
                act.wait_ge(y_copied, n)
                act.dma_start(out[bass.ds(block_row * P, P), :].rearrange("b o -> o b"), yrow[:, :]).then_inc(y_stored, 16)

            act.wait_ge(hot_zeroed, 2)
            for n, group in enumerate(HOT):
                act.wait_ge(hot_loaded[n], 16 * len(group))
                for t in group:
                    if t % 2:
                        act.activation(hot_odd[:, odd_at[t]:odd_at[t] + hot_c[t], DIM:2 * DIM], hot_rows[t], ACT.Copy).then_inc(hot_shifted, 1)
            act.wait_ge(hot_mm, EVEN_GROUPS)
            act.activation(x0t[:, :, :], hot_ps[0], ACT.Copy).then_inc(hot_copied, 1)
            store_x0(0)
            act.wait_ge(zeroed, 1 + len(zero_list))
            act.wait_ge(wt_loaded, 7 * 16)
            def keep_repeat(h):
                act.wait_ge(repeated, h + 1)
                cols = slice(CH * (h % 2), CH * (h % 2 + 1))
                act.activation(bc[:, bc_slot(0, MADE), h // 2, cols], x_ps[:, 1, cols], ACT.Copy).then_inc(bc_loaded[bc_slot(0, MADE)], made_inc)

            for h in range(6):
                keep_repeat(h)
            act.wait_ge(contracted, L0U + 1)
            keep(0, 0)
            spread(0, 0)
            for h in (6, 7):
                keep_repeat(h)

            def body(i, c):
                evac(i, c, "L1a")
                if not c.first:
                    top1(i)
                evac(i, c, "L0b")
                if not c.last:
                    act.wait_ge(x0_stored, 2 * 16 * (i + 1))
                    copy_x0(i + 1)
                    store_x0(i + 1)
                evac(i, c, "L2a")
                act.wait_ge(dense_transposed, i + 1)
                if not c.first:
                    act.wait_ge(h1_mm, i)
                act.activation(dense_t[:, :], m_ps[0:DENSE, 1, :], ACT.Copy).then_inc(dense_ready, 1)
                evac(i, c, "L1b")
                if not c.first:
                    top2(i)
                if not c.last:
                    evac(i, c, "L0c")
                if not c.first:
                    top3(i, i - 1)
                evac(i, c, "L2b")
                if not c.first:
                    act.wait_ge(y_stored, 16 * i)

            body(0, FIRST_BODY)
            with act.Fori(1, TILES - 1) as i:
                body(i, BODY)
            body(TILES - 1, LAST)
            top1(TILES)
            top2(TILES)
            top3(TILES, TILES - 1)

        @block.tensor
        def _(pe):
            def tile_mms(bank, weights, products, start, stop):
                for c in range(2):
                    op = pe.matmul(y_ps[HID * c:HID * (c + 1), bank, :], weights, products[:, CH * c:CH * (c + 1)],
                                   start=start, stop=stop)
                return op

            def keep_warm(n):
                for _ in range(n):
                    pe.matmul(x_ps[:, 0, 0:CH], wl[:, 1, 0:2, :].rearrange("p t k -> p (t k)"), wl[:, 0, 0:CH // HID, :], start=True, stop=True)

            def l0_job(first, p, slot0, bank):
                for n in range(L0U):
                    pe.wait_ge(z_made, first + n + 1)
                    for t in range(UNIT):
                        op = tile_mms(bank, w0s[:, UNIT * n + t, :], z[:, (slot0 + n) % ZR, t, :], n == 0 and t == 0, False)
                    op.then_inc(contracted, 1)
                pe.wait_ge(z16_made, p + 1)
                tile_mms(bank, w16s[:, :], z16[:, :], False, True).then_inc(contracted, 1)

            def transposes(tile):
                pe.wait_ge(gathered, 16 * (len(COLD) + FIELDS * tile))
                pe.wait_ge(x0t_ready, tile)
                for q in range(4):
                    op = pe.transpose(t_ps[:, q, :], emb[:, P * q:P * (q + 1)], ident[:, :])
                op.then_inc(x0_transposed, 1)

            pe.wait_ge(ident_ready, 1)
            pe.wait_ge(zeroed, 1 + len(zero_list))
            pe.wait_ge(hot_zeroed, 4)
            done = odd = 0
            for n, group in enumerate(HOT):
                done += len(group)
                odd += sum(t % 2 for t in group)
                pe.wait_ge(hot_loaded[n], 16 * len(group))
                if odd:
                    pe.wait_ge(hot_shifted, odd)
                pe.wait_ge(onehot_made, done)
                for c in range(HOT_C):
                    for t in group:
                        if c < hot_c[t]:
                            row, q, upper = hot_place(t)
                            rows = hot_odd[:, odd_at[t] + c, :] if upper else hot_rows[t][:, c, :]
                            width = 2 * DIM if upper else DIM
                            op = pe.matmul(hot_ps[upper][row:row + width, q, :], rows, onehot[t][:, c, :], start=c == 0, stop=c == hot_c[t] - 1)
                op.then_inc(hot_mm, 1)
            pe.wait_ge(w_loaded, 4 * 16)
            transposes(0)
            keep_warm(9)
            pe.wait_ge(w0_summed, 6)
            pe.wait_ge(w_loaded, 4 * 16)
            def repeat(h):
                if h >= 2:
                    pe.wait_ge(bc_loaded[bc_slot(0, MADE)], (h - 1) * made_inc)
                cols = slice(CH * (h % 2), CH * (h % 2 + 1))
                pe.matmul(x_ps[:, 1, cols], pick[:, P * (h // 2):P * (h // 2 + 1)], rep[:, cols], start=True, stop=True).then_inc(repeated, 1)

            def l0_first_tile(t):
                pe.wait_ge(z_made if t % UNIT else first_made, t // UNIT + 1)
                op = tile_mms(0, w0s[:, t, :], z[:, t // UNIT, t % UNIT, :], t == 0, t == 3)
                if t % UNIT:
                    op.then_inc(contracted, 1)

            pe.wait_ge(pick_ready, 2)
            pe.wait_ge(rep_loaded, 16)
            for h in range(3):
                repeat(h)
            l0_first_tile(0)
            repeat(3)
            repeat(4)
            l0_first_tile(1)
            repeat(5)
            pe.wait_ge(z16_made, 1)
            tile_mms(0, w16s[:, :], z16[:, :], False, False).then_inc(contracted, 1)
            l0_first_tile(2)
            l0_first_tile(3)
            repeat(6)
            repeat(7)
            pe.wait_ge(wt_loaded, 7 * 16)
            pe.wait_ge(xdup_ready, 1)

            def mlp1_begin(n):
                pe.wait_ge(y_copied, n - 1)
                pe.wait_ge(zin_ready, 3 * n - 1)
                pe.wait_ge(dense_ready, n)
                for m in range(M1):
                    cols = slice(P * m, P * (m + 1))
                    pe.matmul(m_ps[:, m, :], wt1d[:, cols], dense_t[:, :], start=m == 0, stop=False, skip_group_check=True)
                    for lay in range(2):
                        pe.matmul(m_ps[:, m, :], wt1[:, lay, cols], zin[:, lay, :], start=False, stop=False, skip_group_check=True)

            def mlp1_end(n):
                pe.wait_ge(zin_ready, 3 * n)
                for m in range(M1):
                    op = pe.matmul(m_ps[:, m, :], wt1[:, 2, P * m:P * (m + 1)], zin[:, 2, :], start=False, stop=True, skip_group_check=True)
                op.then_inc(h1_mm, 1)

            def mlp1(n):
                pe.wait_ge(zin_ready, 3 * n)
                pe.wait_ge(dense_ready, n)
                for m in range(M1):
                    cols = slice(P * m, P * (m + 1))
                    for lay in range(3):
                        pe.matmul(m_ps[:, m, :], wt1[:, lay, cols], zin[:, lay, :], start=lay == 0, stop=False)
                    op = pe.matmul(m_ps[:, m, :], wt1d[:, cols], dense_t[:, :], start=False, stop=True)
                op.then_inc(h1_mm, 1)

            def mlp2(n, min_ready):
                pe.wait_ge(h1_ready, n)
                pe.wait_ge(dense_ready, min_ready)
                for m in range(M2):
                    for t in range(M1):
                        op = pe.matmul(m_ps[:, m, :], wt2[:, t, P * m:P * (m + 1)], h1[:, t, :], start=t == 0, stop=t == M1 - 1)
                op.then_inc(h2_mm, 1)

            def mlp3(n):
                pe.wait_ge(h2_ready, n)
                for t in range(M2):
                    op = pe.matmul(m_ps[0:1, 0, :], wt3[:, t:t + 1], h2[:, t, :], start=t == 0, stop=t == M2 - 1)
                op.then_inc(y_mm, 1)

            def dense(i, c):
                pe.wait_ge(dctx_loaded, 16 * (i + 1))
                if not c.first:
                    pe.wait_ge(h1_ready, i)
                pe.transpose(m_ps[0:DENSE, 1, :], dctx[:, :], ident[:, :]).then_inc(dense_transposed, 1)

            def body(i, c):
                def job(name, middle={}):
                    number = c.job_number(name, i)
                    bank = c.jobs.index(name) % 2
                    if not (c.first and name == "L1a"):
                        pe.wait_ge(xs_ready, number - 1)
                    if layer(name) == 0:
                        l0_job(c.dve_before(name, i), pair_of(name, i), L0U + c.dve[name], bank)
                        return
                    for pos, g, half, on_pool, n in c.units(name):
                        if pos in middle:
                            middle[pos]()
                        if on_pool:
                            pe.wait_ge(pz_made, c.pool_before(name, i) + n + 1)
                            src = pz[:, (c.pool[name] + n) % PZR, :, :]
                        else:
                            pe.wait_ge(z_made, c.dve_before(name, i) + n + 1)
                            src = z[:, (L0U + c.dve[name] + n) % ZR, :, :]
                        for t in range(UNIT):
                            op = tile_mms(bank, wl[:, layer(name) - 1, GR * g + UNIT * half + t, :], src[:, t, :],
                                          pos == 0 and t == 0, pos == UPJ - 1 and t == UNIT - 1)
                        op.then_inc(contracted, 1)

                job("L1a")
                if not c.first:
                    mlp1(i)
                job("L0b")
                job("L2a", {} if c.last else {TRANSPOSE_AT: lambda: transposes(i + 1)})
                job("L1b", {4: lambda: dense(i, c)})
                if not c.first:
                    mlp2(i, i + 1)
                if not c.last:
                    job("L0c")
                middle = {} if c.first else {MLP3_AT: lambda: mlp3(i)}
                job("L2b", middle)

            body(0, FIRST_BODY)
            with pe.Fori(1, TILES - 1) as i:
                body(i, BODY)
            body(TILES - 1, LAST)
            mlp1_begin(TILES)
            mlp1_end(TILES)
            keep_warm(1)
            mlp2(TILES, TILES)
            mlp3(TILES)


def kernel(**inputs):
    import numpy as np
    import concourse.bacc as bacc
    from concourse.bass_utils import run_bass_kernel_spmd

    nc = bacc.Bacc("TRN2", target_bir_lowering=False, num_devices=1, dynamic_dma_scratch_size=8192)
    arrays, args = {}, {}
    for name, value in inputs.items():
        a = np.ascontiguousarray(value)
        arrays[f"in_{name}"] = a
        args[name] = nc.dram_tensor(f"in_{name}", a.shape, mybir.dt.from_np(a.dtype), kind="ExternalInput").ap()
    out = nc.dram_tensor("out_0", (BATCH, 1), F32, kind="ExternalOutput").ap()
    program(nc, args["dense_ctx"], args["ids"], [args[f"tbl_{t}"] for t in range(FIELDS)],
            args["W_top1"], args["b_top1"], args["W_top2"], args["b_top2"], args["W_top3"],
            args["L0_rec_W0"], args["L0_rec_W1"], args["L0_rec_W2"], out)
    return run_bass_kernel_spmd(nc, [arrays], core_ids=[0]).results[0]["out_0"]
```
